# Optimizing a Trainium2 kernel written in Bass

```python
import numpy as np
import jax
import jax.numpy as jnp

def _softmax(x, axis=-1):
    return jax.nn.softmax(x, axis=axis)
def _gelu(x):
    return jax.nn.gelu(x, approximate=True)
def _silu(x):
    return jax.nn.silu(x)
def _sigmoid(x):
    return jax.nn.sigmoid(x)
def _layernorm(x, axis=-1, eps=1e-5):
    m = jnp.mean(x, axis=axis, keepdims=True)
    v = jnp.var(x, axis=axis, keepdims=True)
    return (x - m) / jnp.sqrt(v + eps)
def _scatter_add(tgt, idx, src, axis=0):
    return tgt.at[idx].add(src)
def _segment_sum(src, seg, n):
    return jax.ops.segment_sum(src, seg, n)

kernel_name = 'mk_conv_preact_d1_conv_nhwc256_90a124'

def setup_inputs(seed: int = 0):
    np.random.seed(seed)
    _w = jnp.asarray
    def _rec_inputs():
        import jax
        import jax.numpy as jnp
        _gk = jax.random.key(seed)
        x = -0.0003929 + 0.9999 * jax.random.normal(jax.random.fold_in(_gk, 1), (16, 64, 64, 256), jnp.float32)
        return x
    x = _rec_inputs()
    def _L0_conv_setup():
        import jax, jax.numpy as jnp
        import numpy as np
        B, H, W, C = (16, 64, 64, 256)
        key = jax.random.key(seed)
        k1, k2, k3 = jax.random.split(key, 3)
        x = jax.random.normal(k1, (B, H, W, C), dtype=jnp.float32)
        W_qkv = jax.random.normal(k2, (C, 3 * C), dtype=jnp.float32) / np.sqrt(C)
        W_out = jax.random.normal(k3, (C, C), dtype=jnp.float32) / np.sqrt(C)
        b_out = jnp.zeros((C,), dtype=jnp.float32)
        return {'x': x, 'W_qkv': W_qkv, 'W_out': W_out, 'b_out': b_out}
    _L0_conv_all = _L0_conv_setup()
    _L0_conv_in = {k: v for k, v in _L0_conv_all.items() if k in ('W_qkv', 'W_out', 'b_out', )}
    del _L0_conv_all

    return {
        "x": x,
        "L0_conv_W_qkv": _L0_conv_in["W_qkv"],
        "L0_conv_W_out": _L0_conv_in["W_out"],
        "L0_conv_b_out": _L0_conv_in["b_out"],
    }

def reference(x, L0_conv_W_qkv, L0_conv_W_out, L0_conv_b_out):
    import jax
    import jax.numpy as jnp
    def _L0_conv_ref(x, W_qkv, W_out, b_out):
        import jax, jax.numpy as jnp
        import numpy as np
        B, H, W, C = (16, 64, 64, 256)
        b, h, w, c = x.shape
        n = h * w
        qkv = jnp.einsum('bhwc,cd->bhwd', x, W_qkv)
        q, k, v = jnp.split(qkv, 3, axis=-1)
        q = q.reshape(b, n, c).transpose(0, 2, 1)
        k = k.reshape(b, n, c).transpose(0, 2, 1)
        v = v.reshape(b, n, c).transpose(0, 2, 1)
        k = jax.nn.softmax(k, axis=-1)
        context = jnp.einsum('bdn,ben->bde', k, v)
        out = jnp.einsum('bde,bdn->ben', context, q)
        out = out.reshape(b, c, h, w).transpose(0, 2, 3, 1)
        return jnp.einsum('bhwc,cd->bhwd', out, W_out) + b_out

    def _gn(v, G=32, eps=1e-5):
        B_, H_, W_, C_ = v.shape
        g = v.reshape(B_, H_, W_, G, C_ // G)
        m = jnp.mean(g, axis=(1, 2, 4), keepdims=True)
        s = jnp.var(g, axis=(1, 2, 4), keepdims=True)
        return ((g - m) / jnp.sqrt(s + eps)).reshape(v.shape)

    def _ln_c(v, eps=1e-6):
        m = jnp.mean(v, axis=-1, keepdims=True)
        s = jnp.var(v, axis=-1, keepdims=True)
        return (v - m) / jnp.sqrt(s + eps)

    def _ln_t(v, eps=1e-5):
        m = jnp.mean(v, axis=-1, keepdims=True)
        s = jnp.var(v, axis=-1, keepdims=True)
        return (v - m) / jnp.sqrt(s + eps)

    def _to_tokens(v):
        B_, H_, W_, C_ = v.shape
        return v.reshape(B_, H_ * W_, C_)
    def _from_tokens(t, like):
        return t.reshape(like.shape)

    x = x + _L0_conv_ref(_gn(x), L0_conv_W_qkv, L0_conv_W_out, L0_conv_b_out)
    return x


_drawn_inputs = setup_inputs


def setup_inputs(seed=0):
    import zlib

    import numpy as np

    out = dict(_drawn_inputs(seed))
    spreads = {'L0_conv_b_out': (0.0, 0.1)}
    factors = {}
    for name, (base, spread) in spreads.items():
        noise = np.random.default_rng([zlib.crc32(name.encode()), seed]).standard_normal(out[name].shape)
        drawn = base * np.exp(spread * noise) if base else spread * noise
        out[name] = jnp.asarray(drawn.astype(out[name].dtype))
    for name, factor in factors.items():
        out[name] = (out[name] * factor).astype(out[name].dtype)
    return out
```

```python
from contextlib import ExitStack

import concourse.bass as bass
from concourse import mybir

ALU = mybir.AluOpType
ACT = mybir.ActivationFunctionType
AX_X = mybir.AxisListType.X
F32 = mybir.dt.float32
F32R = mybir.dt.float32r

P = 128
GROUPS = 32
EPS = 1e-5
TILES = 4
CH = TILES * P


def build(nc: bass.Bass, x: bass.AP, w_qkv: bass.AP, w_out: bass.AP, b_out: bass.AP, out: bass.AP):
    B, H, W, C = x.shape
    NCH = H * W // CH
    CB = C // P
    GC = C // GROUPS
    assert CB == 2 and NCH == 8 and P % GC == 0

    x_chunks = x.rearrange("b h w c -> (b h w) c").rearrange("(g p t) c -> g p (t c)", p=P, t=TILES)
    out_chunks = out.rearrange("b h w c -> (b h w) c").rearrange("(g p t) c -> g p (t c)", p=P, t=TILES)

    with ExitStack() as ctx:
        def sb(name, shape, dt=F32):
            return ctx.enter_context(nc.sbuf_tensor(name, shape, dt))

        def psum(name, shape):
            return ctx.enter_context(nc.psum_tensor(name, shape, F32))

        def sem(name):
            return ctx.enter_context(nc.semaphore(name))

        x_nat = sb("x_nat", [P, NCH, TILES * C])
        xt_hi = sb("xt_hi", [P, NCH, CB, CH], F32R)
        xt_lo = sb("xt_lo", [P, NCH, CB, CH], F32R)
        x_hi = sb("x_hi", [P, 2, TILES * C], F32R)
        x_lo = sb("x_lo", [P, 2, TILES * C], F32R)
        e_dn = sb("e_dn", [P, 2, CB, CH])
        e_hi = sb("e_hi", [P, 2, 2 * C], F32R)
        e_lo = sb("e_lo", [P, 2, 2 * C], F32R)
        o_stage = sb("o_stage", [P, 2, TILES * C])
        wqkv = sb("wqkv", [P, CB, 3 * C])
        wo = sb("wo", [P, CB, C])
        wv_t = sb("wv_t", [P, CB, C])
        wq_t = sb("wq_t", [P, CB, C])
        wvo = sb("wvo", [P, CB, C])
        wq_sum = sb("wq_sum", [P, C])
        b_row = sb("b_row", [1, C])
        b_tile = sb("b_tile", [P, C])
        ones = sb("ones", [P, P])
        ident = sb("ident", [P, P])
        eye = sb("eye", [P, CB, C])
        grp = sb("grp", [P, P])
        neg_half = sb("neg_half", [P, CB])
        bn = sb("bn", [P, CB, NCH, 6])
        mv = sb("mv", [P, CB, 2])
        wait_holder = sb("wait_holder", [P, 1])
        dev = sb("dev", [P, CB])
        dev2 = sb("dev2", [P, CB])
        var2 = sb("var2", [P, CB])
        neg_mean = sb("neg_mean", [P, CB])
        var_eps = sb("var_eps", [P, CB])
        rstd = sb("rstd", [P, CB])
        neg_mean_bc = sb("neg_mean_bc", [P, CB, P])
        wk_hi = sb("wk_hi", [P, CB, C], F32R)
        wk_lo = sb("wk_lo", [P, CB, C], F32R)
        wvo_r = sb("wvo_r", [P, CB, C])
        cmax = sb("cmax", [P, NCH, CB])
        neg_max = sb("neg_max", [P, NCH, CB])
        max_step = sb("max_step", [P, NCH, CB])
        alpha = sb("alpha", [P, NCH, CB])
        e_sum = sb("e_sum", [P, NCH, CB])
        z = sb("z", [P, CB])
        z_old = sb("z_old", [P, NCH, CB])
        rz = sb("rz", [P, CB])
        acc = sb("acc", [P, CB, C])
        u_sb = sb("u_sb", [P, CB, C])
        m_full = sb("m_full", [P, CB, C])
        m_hi = sb("m_hi", [P, CB, C], F32R)
        m_lo = sb("m_lo", [P, CB, C], F32R)
        m_diff = sb("m_diff", [P, CB, C])
        bias = sb("bias", [P, C])

        ps_k = psum("ps_k", [P, 2, CB, CH])
        ps_t = psum("ps_t", [P, 2, 2 * C])
        ps_a = psum("ps_a", [P, CB, C])
        ps_s = psum("ps_s", [P, 2 * C])

        w_loaded = sem("w_loaded")
        x_loaded = [sem(f"x_loaded{p}") for p in range(NCH)]
        stored = [sem(f"stored{i}") for i in range(2)]
        filled = sem("filled")
        eye_zero = sem("eye_zero")
        consts_ready = sem("consts_ready")
        eye_ready = sem("eye_ready")
        setup_ps = sem("setup_ps")
        setup_sb = sem("setup_sb")
        xt_ps_ready = sem("xt_ps_ready")
        xt_hi_ready = sem("xt_hi_ready")
        xt_lo_ready = sem("xt_lo_ready")
        mv_ready = sem("mv_ready")
        mean_ps = sem("mean_ps")
        mean_read = sem("mean_read")
        dev2_ready = sem("dev2_ready")
        var2_ready = sem("var2_ready")
        var_ps = sem("var_ps")
        var_eps_ready = sem("var_eps_ready")
        rstd_ready = sem("rstd_ready")
        wk_hi_ready = sem("wk_hi_ready")
        wk_ready = sem("wk_ready")
        scaled_ready = sem("scaled_ready")
        k_ready = sem("k_ready")
        cmax_ready = sem("cmax_ready")
        shift_ready = sem("shift_ready")
        step_ready = sem("step_ready")
        alpha_ready = sem("alpha_ready")
        e_ready = sem("e_ready")
        et_ready = sem("et_ready")
        e_hi_ready = sem("e_hi_ready")
        e_lo_ready = sem("e_lo_ready")
        x_hi_ready = sem("x_hi_ready")
        x_lo_ready = sem("x_lo_ready")
        a_ready = sem("a_ready")
        a_added = sem("a_added")
        z_old_ready = sem("z_old_ready")
        z_ready = sem("z_ready")
        rz_ready = sem("rz_ready")
        a_norm = sem("a_norm")
        u_ps = sem("u_ps")
        u_ready = sem("u_ready")
        m_ps = sem("m_ps")
        m_full_ready = sem("m_full_ready")
        m_hi_ready = sem("m_hi_ready")
        m_ready = sem("m_ready")
        m_diff_ready = sem("m_diff_ready")
        bias_ps = sem("bias_ps")
        bias_ready = sem("bias_ready")
        r_ready = sem("r_ready")
        o_ready = sem("o_ready")

        halves = ((0, 0), (0, 1), (1, 0))

        block = ctx.enter_context(nc.Block())

        @block.sync
        def _(sp):
            sp.dma_start(x_nat[:, 0, :], x_chunks[0]).then_inc(x_loaded[0], 16)
            sp.dma_start(wqkv[:], w_qkv.rearrange("(j p) n -> p j n", p=P)).then_inc(w_loaded, 16)
            sp.dma_start(wo[:], w_out.rearrange("(j p) n -> p j n", p=P)).then_inc(w_loaded, 16)
            sp.dma_start(b_row[:], b_out.rearrange("(a n) -> a n", a=1)).then_inc(w_loaded, 16)
            for p in range(1, NCH):
                sp.dma_start(x_nat[:, p, :], x_chunks[p]).then_inc(x_loaded[p], 16)

            def load_image(b):
                for p in range(NCH):
                    sp.wait_ge(x_lo_ready, b * NCH + (p + 1))
                    sp.dma_start(x_nat[:, p, :], x_chunks[bass.ds(b * NCH + (NCH + p), 1)].rearrange(
                        "a p n -> (a p) n")).then_inc(x_loaded[p], 16)

            def store_image(b):
                for p in range(NCH):
                    sp.wait_ge(o_ready, b * NCH + (p + 1))
                    sp.dma_start(out_chunks[bass.ds(b * NCH + p, 1)].rearrange("a p n -> (a p) n"),
                                 o_stage[:, p % 2, :]).then_inc(stored[p % 2], 16)

            with sp.Fori(0, B - 1) as b:
                load_image(b)
                store_image(b)
            store_image(B - 1)
            for s in stored:
                sp.wait_ge(s, 16 * (B * NCH // 2 + 1))

        @block.gpsimd
        def _(pool):
            nc.gpsimd.memset(ones[:], 1.0).then_inc(consts_ready, 1)
            nc.gpsimd.memset(neg_half[:], -0.5).then_inc(consts_ready, 1)
            nc.gpsimd.memset(ident[:], 0.0).then_inc(filled, 1)
            pool.wait_ge(filled, 1)
            nc.gpsimd.affine_select(out=ident[:], in_=ident[:], compare_op=ALU.not_equal, fill=1.0, base=0,
                                    pattern=[[-1, P]], channel_multiplier=1).then_inc(consts_ready, 1)
            nc.gpsimd.memset(grp[:], 1.0 / GC).then_inc(filled, 1)
            pool.wait_ge(filled, 2)
            g3 = grp[:].rearrange("p (g i) -> p g i", i=GC)
            nc.gpsimd.affine_select(out=g3, in_=g3, compare_op=ALU.is_ge, fill=0.0, base=0,
                                    pattern=[[-GC, P // GC], [0, GC]], channel_multiplier=1).then_inc(filled, 1)
            pool.wait_ge(filled, 3)
            nc.gpsimd.affine_select(out=g3, in_=g3, compare_op=ALU.is_ge, fill=0.0, base=GC - 1,
                                    pattern=[[GC, P // GC], [0, GC]], channel_multiplier=-1).then_inc(consts_ready, 1)

            def rstd_of(b):
                pool.wait_ge(var_eps_ready, b + 1)
                nc.gpsimd.tensor_tensor(rstd[:], var_eps[:], neg_half[:], ALU.pow).then_inc(rstd_ready, 1)

            rstd_of(0)
            with pool.Fori(0, B - 1) as b:
                rstd_of(b + 1)

        @block.tensor
        def _(pe):
            def turn(b, p):
                pe.wait_ge(x_loaded[p], b * 16 + 16)
                if not (isinstance(b, int) and b == 0 and p == 0):
                    pe.wait_ge(xt_lo_ready, b * NCH + p)
                for c in range(CB):
                    for t in range(TILES):
                        last = nc.tensor.transpose(ps_t[:, c, t * P:(t + 1) * P],
                                                   x_nat[:, p, t * C + c * P:t * C + (c + 1) * P], ident[:])
                last.then_inc(xt_ps_ready, 1)

            def stats(b):
                pe.wait_ge(mv_ready, b + 1)
                nc.tensor.matmul(ps_s[:, 0:CB], grp[:], mv[:, :, 0], start=True, stop=True).then_inc(mean_ps, 1)
                pe.wait_ge(var2_ready, b + 1)
                nc.tensor.matmul(ps_s[:, CB:2 * CB], grp[:], var2[:], start=True, stop=True).then_inc(var_ps, 1)

            def keys(b, j):
                for d in range(CB):
                    n = 0
                    for ws, xs in halves:
                        for c in range(CB):
                            last = nc.tensor.matmul(ps_k[:, j % 2, d, :],
                                                    (wk_hi, wk_lo)[ws][:, c, d * P:(d + 1) * P],
                                                    (xt_hi, xt_lo)[xs][:, j, c, :],
                                                    start=(n == 0), stop=(n == 3 * CB - 1))
                            n += 1
                last.then_inc(k_ready, 1)

            def turn_e(b, j, h):
                for u in range(2):
                    t = 2 * h + u
                    for d in range(CB):
                        last = nc.tensor.transpose(ps_t[:, h, u * C + d * P:u * C + (d + 1) * P],
                                                   e_dn[:, j % 2, d, t * P:(t + 1) * P], ident[:])
                last.then_inc(et_ready, 1)

            def gather(b, j, h):
                pe.wait_ge(e_lo_ready, b * (2 * NCH) + (2 * j + h + 1))
                if h == 0:
                    pe.wait_ge(x_lo_ready, b * NCH + (j + 1))
                    if j >= 1:
                        pe.wait_ge(a_added, b * NCH + j)
                for u in range(2):
                    t = 2 * h + u
                    for d in range(CB):
                        for n, (es, xs) in enumerate(halves):
                            first = h == 0 and u == 0 and d == 0 and n == 0
                            final = h == 1 and u == 1 and n == 2
                            last = nc.tensor.matmul(ps_a[:, d, :],
                                                    (e_hi, e_lo)[es][:, h, u * C + d * P:u * C + (d + 1) * P],
                                                    (x_hi, x_lo)[xs][:, j % 2, t * C:(t + 1) * C],
                                                    start=first, stop=final, skip_group_check=True)
                if h == 1:
                    last.then_inc(a_ready, 1)

            def attend(b):
                pe.wait_ge(wk_ready, b + 1)
                pe.wait_ge(xt_lo_ready, b * NCH + NCH)
                keys(b, 0)
                for j in range(NCH):
                    if j + 1 < NCH:
                        if j >= 1:
                            pe.wait_ge(e_ready, b * NCH + j)
                        keys(b, j + 1)
                    pe.wait_ge(e_ready, b * NCH + (j + 1))
                    if j >= 1:
                        pe.wait_ge(e_lo_ready, b * (2 * NCH) + (2 * j - 1))
                    turn_e(b, j, 0)
                    if j >= 1:
                        gather(b, j - 1, 1)
                    turn_e(b, j, 1)
                    gather(b, j, 0)
                gather(b, NCH - 1, 1)

            def combine(b):
                pe.wait_ge(a_norm, b + 1)
                for c in range(CB):
                    for d in range(CB):
                        last = nc.tensor.matmul(ps_s[:, c * C:(c + 1) * C], acc[:, d, c * P:(c + 1) * P],
                                                wq_t[:, d, :], start=(c == 0 and d == 0), stop=(d == CB - 1),
                                                skip_group_check=True)
                last.then_inc(u_ps, 1)
                pe.wait_ge(u_ready, b + 1)
                pe.wait_ge(scaled_ready, b + 1)
                for i in range(CB):
                    for c in range(CB):
                        last = nc.tensor.matmul(ps_a[:, i, :], u_sb[:, c, i * P:(i + 1) * P], wvo_r[:, c, :],
                                                start=(i == 0 and c == 0), stop=(c == CB - 1),
                                                skip_group_check=True)
                last.then_inc(m_ps, 1)

            def bias_row(b):
                pe.wait_ge(m_diff_ready, b + 1)
                for c in range(CB):
                    last = nc.tensor.matmul(ps_s[:, 0:C], neg_mean_bc[:, c, :], m_diff[:, c, :],
                                            start=(c == 0), stop=(c == CB - 1))
                last.then_inc(bias_ps, 1)

            def emit(b, p):
                if p == 0:
                    pe.wait_ge(m_ready, b + 1)
                if p >= 2:
                    pe.wait_ge(o_ready, b * NCH + (p - 1))
                for t in range(TILES):
                    n = 0
                    for xs, ms in halves:
                        for c in range(CB):
                            last = nc.tensor.matmul(ps_k[:, p % 2, t // 2, (t % 2) * C:(t % 2 + 1) * C],
                                                    (xt_hi, xt_lo)[xs][:, p, c, t * P:(t + 1) * P],
                                                    (m_hi, m_lo)[ms][:, c, :],
                                                    start=(t % 2 == 0 and n == 0), stop=(n == 3 * CB - 1),
                                                    skip_group_check=True)
                            n += 1
                last.then_inc(r_ready, 1)

            pe.wait_ge(consts_ready, 4)
            pe.wait_ge(w_loaded, 48)
            for i, first_col in enumerate((0, 2 * C)):
                for n in range(CB):
                    for c in range(CB):
                        last = nc.tensor.transpose(
                            ps_k[:, i, n, c * P:(c + 1) * P],
                            wqkv[:, c, first_col + n * P:first_col + (n + 1) * P], ident[:])
                last.then_inc(setup_ps, 1)
            pe.wait_ge(setup_sb, 2)
            for c in range(CB):
                for e in range(CB):
                    last = nc.tensor.matmul(ps_k[:, 0, c, 0:C], wv_t[:, e, c * P:(c + 1) * P], wo[:, e, :],
                                            start=(e == 0), stop=(e == CB - 1))
            last.then_inc(setup_ps, 1)
            for d in range(CB):
                nc.tensor.matmul(ps_k[:, 1, 0, 0:C], ones[:], wq_t[:, d, :], start=(d == 0), stop=(d == CB - 1))
            nc.tensor.matmul(ps_k[:, 1, 1, 0:C], ones[0:1, :], b_row[:], start=True, stop=True).then_inc(setup_ps, 1)

            for p in range(NCH):
                turn(0, p)
            stats(0)
            pe.wait_ge(setup_sb, 5)
            with pe.Fori(0, B - 1) as b:
                attend(b)
                combine(b)
                for p in range(NCH):
                    emit(b, p)
                    if p == 0:
                        bias_row(b)
                    turn(b + 1, p)
                stats(b + 1)
            attend(B - 1)
            combine(B - 1)
            for p in range(NCH):
                emit(B - 1, p)
                if p == 0:
                    bias_row(B - 1)

        @block.scalar
        def _(act):
            def turn(b, p):
                act.wait_ge(xt_ps_ready, b * NCH + (p + 1))
                nc.scalar.activation(xt_hi[:, p, :, :], ps_t[:], ACT.Copy).then_inc(xt_hi_ready, 1)

            def e_high(b, j, h):
                act.wait_ge(et_ready, b * (2 * NCH) + (2 * j + h + 1))
                nc.scalar.activation(e_hi[:, h, :], ps_t[:, h, :], ACT.Copy).then_inc(e_hi_ready, 1)

            def x_high(b, j):
                if j >= 2:
                    act.wait_ge(a_ready, b * NCH + (j - 1))
                nc.scalar.activation(x_hi[:, j % 2, :], x_nat[:, j, :], ACT.Copy).then_inc(x_hi_ready, 1)

            def exps(b, j):
                act.wait_ge(shift_ready, b * NCH + (j + 1))
                for d in range(CB):
                    last = nc.scalar.activation(e_dn[:, j % 2, d, :], ps_k[:, j % 2, d, :], ACT.Exp,
                                                bias=neg_max[:, j, d:d + 1], accum_out=e_sum[:, j, d:d + 1])
                last.then_inc(e_ready, 1)
                if j >= 1:
                    act.wait_ge(step_ready, b * (NCH - 1) + j)
                    nc.scalar.activation(alpha[:, j, :], max_step[:, j, :], ACT.Exp).then_inc(alpha_ready, 1)

            def attend(b):
                for j in range(NCH):
                    if j >= 1:
                        e_high(b, j - 1, 0)
                        e_high(b, j - 1, 1)
                    if j == 0:
                        for p in range(NCH):
                            act.wait_ge(x_loaded[p], b * 16 + 16)
                    x_high(b, j)
                    exps(b, j)
                e_high(b, NCH - 1, 0)
                e_high(b, NCH - 1, 1)

            for p in range(NCH):
                turn(0, p)
            with act.Fori(0, B - 1) as b:
                attend(b)
                for p in range(NCH):
                    turn(b + 1, p)
            attend(B - 1)

        @block.vector
        def _(dve):
            def turn(b, p):
                dve.wait_ge(xt_hi_ready, b * NCH + (p + 1))
                for c in range(CB):
                    nc.vector.bn_stats(bn[:, c, p, :], ps_t[:, c, :])
                nc.vector.tensor_tensor(xt_lo[:, p, :, :], ps_t[:], xt_hi[:, p, :, :].bitcast(F32),
                                        ALU.subtract).then_inc(xt_lo_ready, 1)

            def stats(b):
                dve.wait_ge(xt_lo_ready, b * NCH + NCH)
                nc.vector.memset(wait_holder[:], 0.0)
                for c in range(CB):
                    last = nc.vector.bn_aggr(mv[:, c, :], bn[:, c, :, :].rearrange("p k s -> p (k s)"))
                last.then_inc(mv_ready, 1)
                dve.wait_ge(mean_ps, b + 1)
                nc.vector.tensor_tensor(dev[:], mv[:, :, 0], ps_s[:, 0:CB], ALU.subtract)
                nc.vector.tensor_scalar(neg_mean[:], ps_s[:, 0:CB], -1.0, None, ALU.mult).then_inc(mean_read, 1)
                dve.wait_ge(mean_read, b + 1)
                nc.vector.tensor_tensor(dev2[:], dev[:], dev[:], ALU.mult).then_inc(dev2_ready, 1)
                dve.wait_ge(dev2_ready, b + 1)
                nc.vector.tensor_tensor(var2[:], dev2[:], mv[:, :, 1], ALU.add).then_inc(var2_ready, 1)
                dve.wait_ge(var_ps, b + 1)
                nc.vector.tensor_scalar(var_eps[:], ps_s[:, CB:2 * CB], EPS, None, ALU.add).then_inc(var_eps_ready, 1)
                dve.wait_ge(rstd_ready, b + 1)
                for c in range(CB):
                    last = nc.vector.tensor_scalar(wk_hi[:, c, :], wqkv[:, c, C:2 * C], rstd[:, c:c + 1], None,
                                                   ALU.mult)
                last.then_inc(wk_hi_ready, 1)
                dve.wait_ge(wk_hi_ready, b + 1)
                for c in range(CB):
                    last = nc.vector.scalar_tensor_tensor(out=wk_lo[:, c, :], in0=wqkv[:, c, C:2 * C],
                                                          scalar=rstd[:, c:c + 1], in1=wk_hi[:, c, :].bitcast(F32),
                                                          op0=ALU.mult, op1=ALU.subtract)
                last.then_inc(wk_ready, 1)
                for c in range(CB):
                    nc.vector.tensor_scalar(wvo_r[:, c, :], wvo[:, c, :], rstd[:, c:c + 1], None, ALU.mult)
                    last = nc.vector.tensor_scalar(neg_mean_bc[:, c, :], ones[:], neg_mean[:, c:c + 1], None,
                                                   ALU.mult)
                last.then_inc(scaled_ready, 1)

            def chunk_max(b, j):
                dve.wait_ge(k_ready, b * NCH + (j + 1))
                nc.vector.tensor_reduce(cmax[:, j, :], ps_k[:, j % 2, :, :], AX_X, ALU.max).then_inc(cmax_ready, 1)

            def shift(b, j):
                dve.wait_ge(cmax_ready, b * NCH + (j + 1))
                if j == 0:
                    nc.vector.tensor_scalar(neg_max[:, 0, :], cmax[:, 0, :], -1.0, None, ALU.mult).then_inc(shift_ready, 1)
                    return
                nc.vector.scalar_tensor_tensor(out=neg_max[:, j, :], in0=cmax[:, j, :], scalar=-1.0,
                                               in1=neg_max[:, j - 1, :], op0=ALU.mult,
                                               op1=ALU.min).then_inc(shift_ready, 1)
                dve.wait_ge(shift_ready, b * NCH + (j + 1))
                nc.vector.tensor_tensor(max_step[:, j, :], neg_max[:, j, :], neg_max[:, j - 1, :],
                                        ALU.subtract).then_inc(step_ready, 1)

            def e_low(b, j, h):
                dve.wait_ge(e_hi_ready, b * (2 * NCH) + (2 * j + h + 1))
                nc.vector.tensor_tensor(e_lo[:, h, :], ps_t[:, h, :], e_hi[:, h, :].bitcast(F32),
                                        ALU.subtract).then_inc(e_lo_ready, 1)

            def add_a(b, j):
                dve.wait_ge(a_ready, b * NCH + (j + 1))
                if j == 0:
                    nc.vector.tensor_copy(z[:], e_sum[:, 0, :]).then_inc(z_ready, 1)
                    nc.vector.tensor_copy(acc[:], ps_a[:]).then_inc(a_added, 1)
                    return
                dve.wait_ge(alpha_ready, b * (NCH - 1) + j)
                dve.wait_ge(a_added, b * NCH + j)
                nc.vector.tensor_tensor(z_old[:, j, :], z[:], alpha[:, j, :], ALU.mult).then_inc(z_old_ready, 1)
                for d in range(CB):
                    last = nc.vector.scalar_tensor_tensor(out=acc[:, d, :], in0=acc[:, d, :],
                                                          scalar=alpha[:, j, d:d + 1], in1=ps_a[:, d, :],
                                                          op0=ALU.mult, op1=ALU.add)
                last.then_inc(a_added, 1)
                dve.wait_ge(z_old_ready, b * (NCH - 1) + j)
                nc.vector.tensor_tensor(z[:], z_old[:, j, :], e_sum[:, j, :], ALU.add).then_inc(z_ready, 1)

            def x_low(b, j):
                dve.wait_ge(x_hi_ready, b * NCH + (j + 1))
                nc.vector.tensor_tensor(x_lo[:, j % 2, :], x_nat[:, j, :], x_hi[:, j % 2, :].bitcast(F32),
                                        ALU.subtract).then_inc(x_lo_ready, 1)

            def attend(b):
                for j in range(NCH):
                    chunk_max(b, j)
                    if j >= 1:
                        e_low(b, j - 1, 0)
                    shift(b, j)
                    if j >= 2:
                        add_a(b, j - 2)
                    if j >= 1:
                        e_low(b, j - 1, 1)
                    x_low(b, j)
                e_low(b, NCH - 1, 0)
                add_a(b, NCH - 2)
                e_low(b, NCH - 1, 1)
                add_a(b, NCH - 1)

            def combine(b):
                dve.wait_ge(z_ready, b * NCH + NCH)
                nc.vector.reciprocal(rz[:], z[:]).then_inc(rz_ready, 1)
                dve.wait_ge(rz_ready, b + 1)
                for d in range(CB):
                    last = nc.vector.tensor_scalar(acc[:, d, :], acc[:, d, :], rz[:, d:d + 1], None, ALU.mult)
                last.then_inc(a_norm, 1)
                dve.wait_ge(u_ps, b + 1)
                for c in range(CB):
                    last = nc.vector.scalar_tensor_tensor(out=u_sb[:, c, :], in0=wq_sum[:],
                                                          scalar=neg_mean[:, c:c + 1],
                                                          in1=ps_s[:, c * C:(c + 1) * C],
                                                          op0=ALU.mult, op1=ALU.add)
                last.then_inc(u_ready, 1)
                dve.wait_ge(m_ps, b + 1)
                for i in range(CB):
                    last = nc.vector.scalar_tensor_tensor(out=m_full[:, i, :], in0=ps_a[:, i, :],
                                                          scalar=rstd[:, i:i + 1], in1=eye[:, i, :],
                                                          op0=ALU.mult, op1=ALU.add)
                last.then_inc(m_full_ready, 1)
                dve.wait_ge(m_full_ready, b + 1)
                nc.vector.tensor_copy(m_hi[:], m_full[:]).then_inc(m_hi_ready, 1)
                dve.wait_ge(m_hi_ready, b + 1)
                nc.vector.tensor_tensor(m_lo[:], m_full[:], m_hi[:].bitcast(F32), ALU.subtract).then_inc(m_ready, 1)
                nc.vector.tensor_tensor(m_diff[:], m_full[:], eye[:], ALU.subtract).then_inc(m_diff_ready, 1)

            def bias_row(b):
                dve.wait_ge(bias_ps, b + 1)
                nc.vector.tensor_tensor(bias[:], ps_s[:, 0:C], b_tile[:], ALU.add).then_inc(bias_ready, 1)
                dve.wait_ge(bias_ready, b + 1)

            def emit(b, p):
                if p == 0:
                    bias_row(b)
                dve.wait_ge(r_ready, b * NCH + (p + 1))
                dve.wait_ge(stored[p % 2], b * (16 * NCH // 2) + 16 * (p // 2 + 1))
                nc.vector.tensor_tensor(
                    o_stage[:, p % 2, :].rearrange("p (t c) -> p t c", t=TILES),
                    ps_k[:, p % 2, :, :].rearrange("p g (u c) -> p (g u) c", u=2),
                    bias[:].unsqueeze(1).broadcast_to([P, TILES, C]), ALU.add).then_inc(o_ready, 1)

            for s in stored:
                dve.sem_inc(s, 16)
            nc.vector.memset(eye[:], 0.0).then_inc(eye_zero, 1)
            dve.wait_ge(eye_zero, 1)
            dve.wait_ge(consts_ready, 4)
            for c in range(CB):
                last = nc.vector.tensor_copy(eye[:, c, c * P:(c + 1) * P], ident[:])
            last.then_inc(eye_ready, 1)
            for i, to in enumerate((wq_t, wv_t)):
                dve.wait_ge(setup_ps, i + 1)
                nc.vector.tensor_copy(to[:], ps_k[:, i, :, 0:C]).then_inc(setup_sb, 1)
            dve.wait_ge(setup_ps, 3)
            nc.vector.tensor_copy(wvo[:], ps_k[:, 0, :, 0:C]).then_inc(setup_sb, 1)
            dve.wait_ge(setup_ps, 4)
            nc.vector.tensor_copy(wq_sum[:], ps_k[:, 1, 0, 0:C]).then_inc(setup_sb, 1)
            nc.vector.tensor_copy(b_tile[:], ps_k[:, 1, 1, 0:C]).then_inc(setup_sb, 1)
            dve.wait_ge(setup_sb, 5)
            dve.wait_ge(eye_ready, 1)

            for p in range(NCH):
                turn(0, p)
            stats(0)
            with dve.Fori(0, B - 1) as b:
                attend(b)
                combine(b)
                for p in range(NCH):
                    emit(b, p)
                    turn(b + 1, p)
                stats(b + 1)
            attend(B - 1)
            combine(B - 1)
            for p in range(NCH):
                emit(B - 1, p)


_INS = ["x", "L0_conv_W_qkv", "L0_conv_W_out", "L0_conv_b_out"]


def kernel(**inputs):
    import numpy as np
    import concourse.bacc as bacc
    from concourse.bass_utils import run_bass_kernel_spmd

    nc = bacc.Bacc("TRN2", target_bir_lowering=False, num_devices=1)
    arrays, args = {}, []
    for name in _INS:
        a = np.ascontiguousarray(inputs[name])
        arrays[f"in_{name}_dram"] = a
        args.append(nc.dram_tensor(f"in_{name}_dram", a.shape, mybir.dt.from_np(a.dtype), kind="ExternalInput").ap())
    o = nc.dram_tensor("out_0_dram", inputs["x"].shape, F32, kind="ExternalOutput").ap()
    build(nc, *args, o)
    r = run_bass_kernel_spmd(nc, [arrays], core_ids=[0])
    return r.results[0]["out_0_dram"]
```

```python
from contextlib import ExitStack

import concourse.bass as bass
from concourse import mybir

ALU = mybir.AluOpType
ACT = mybir.ActivationFunctionType
AX_X = mybir.AxisListType.X
F32 = mybir.dt.float32
F32R = mybir.dt.float32r

P = 128
GROUPS = 32
EPS = 1e-5
TILES = 4
CH = TILES * P
LATE = (6, 7)
TURN_ORDER = (0, 4, 1, 5, 2, 3, 6, 7)
DOUBLED = (0, 4, 5, 6, 7)


def build(nc: bass.Bass, x: bass.AP, w_qkv: bass.AP, w_out: bass.AP, b_out: bass.AP, out: bass.AP):
    B, H, W, C = x.shape
    NCH = H * W // CH
    CB = C // P
    GC = C // GROUPS
    assert CB == 2 and NCH == 8 and P % GC == 0

    x_chunks = x.rearrange("b h w c -> (b h w) c").rearrange("(g p t) c -> g p (t c)", p=P, t=TILES)
    out_chunks = out.rearrange("b h w c -> (b h w) c").rearrange("(g p t) c -> g p (t c)", p=P, t=TILES)

    with ExitStack() as ctx:
        def sb(name, shape, dt=F32):
            return ctx.enter_context(nc.sbuf_tensor(name, shape, dt))

        def psum(name, shape):
            return ctx.enter_context(nc.psum_tensor(name, shape, F32))

        def sem(name):
            return ctx.enter_context(nc.semaphore(name))

        x_nat = sb("x_nat", [P, NCH, TILES * C])
        xt_hi = sb("xt_hi", [P, NCH + len(DOUBLED), CB, CH], F32R)
        xt_lo = sb("xt_lo", [P, NCH + len(DOUBLED), CB, CH], F32R)
        x_hi = sb("x_hi", [P, 2, TILES * C], F32R)
        x_lo = sb("x_lo", [P, 2, TILES * C], F32R)
        e_dn = sb("e_dn", [P, 2, CB, CH])
        e_hi = sb("e_hi", [P, 2, 2 * C], F32R)
        e_lo = sb("e_lo", [P, 2, 2 * C], F32R)
        o_stage = sb("o_stage", [P, 2, TILES * C])
        w_stage = e_dn[:].rearrange("p a d n -> p (a d n)")
        wqkv = w_stage[:, 0:CB * 3 * C].rearrange("p (j n) -> p j n", j=CB)
        wo = w_stage[:, CB * 3 * C:CB * 4 * C].rearrange("p (j n) -> p j n", j=CB)
        wk = sb("wk", [P, CB, C])
        wq_t = sb("wq_t", [P, CB, C])
        wvo = sb("wvo", [P, CB, C])
        wq_sum = sb("wq_sum", [P, C])
        b_row = sb("b_row", [1, C])
        b_tile = sb("b_tile", [P, C])
        ones = sb("ones", [P, P])
        zero_eye = sb("zero_eye", [P, 3 * P])
        ident = zero_eye[:, P:2 * P]
        eye = [zero_eye[:, P:3 * P], zero_eye[:, 0:2 * P]]
        grp = sb("grp", [P, P])
        neg_half = sb("neg_half", [P, CB])
        bn = sb("bn", [P, CB, NCH, 6])
        mv = sb("mv", [P, CB, 2])
        wait_holder = sb("wait_holder", [P, 1])
        dev = sb("dev", [P, CB])
        dev2 = sb("dev2", [P, CB])
        var2 = sb("var2", [P, CB])
        neg_mean = sb("neg_mean", [P, CB])
        var_eps = sb("var_eps", [P, CB])
        rstd = sb("rstd", [P, CB])
        neg_mean_bc = sb("neg_mean_bc", [P, CB, P])
        wk_hi = sb("wk_hi", [P, CB, C], F32R)
        wk_lo = sb("wk_lo", [P, CB, C], F32R)
        wvo_r = sb("wvo_r", [P, CB, C])
        cmax = sb("cmax", [P, NCH, CB])
        neg_max = sb("neg_max", [P, NCH, CB])
        max_step = sb("max_step", [P, NCH, CB])
        alpha = sb("alpha", [P, NCH, CB])
        e_sum = sb("e_sum", [P, NCH, CB])
        z = sb("z", [P, CB])
        z_old = sb("z_old", [P, NCH, CB])
        rz = sb("rz", [P, CB])
        acc = sb("acc", [P, CB, C])
        u_sb = sb("u_sb", [P, CB, C])
        m_full = acc
        m_hi = sb("m_hi", [P, CB, C], F32R)
        m_lo = sb("m_lo", [P, CB, C], F32R)
        m_diff = u_sb
        wv_t = u_sb
        bias = sb("bias", [P, C])

        ps_k = psum("ps_k", [P, 2, CB, CH])
        ps_t = psum("ps_t", [P, 2, 2 * C])
        ps_a = psum("ps_a", [P, 2, CB * C])
        ps_turn = (ps_t, ps_a)

        w_loaded = sem("w_loaded")
        x_loaded = [sem(f"x_loaded{p}") for p in range(NCH)]
        stored = [sem(f"stored{i}") for i in range(2)]
        filled = sem("filled")
        consts_ready = sem("consts_ready")
        bn_ready = sem("bn_ready")
        r_read = sem("r_read")
        setup_ps = sem("setup_ps")
        setup_sb = sem("setup_sb")
        xt_ps_ready = sem("xt_ps_ready")
        xt_hi_ready = sem("xt_hi_ready")
        xt_lo_ready = sem("xt_lo_ready")
        mv_ready = sem("mv_ready")
        mean_ps = sem("mean_ps")
        mean_read = sem("mean_read")
        dev2_ready = sem("dev2_ready")
        var2_ready = sem("var2_ready")
        var_ps = sem("var_ps")
        var_eps_ready = sem("var_eps_ready")
        rstd_ready = sem("rstd_ready")
        wk_hi_ready = sem("wk_hi_ready")
        wk_ready = sem("wk_ready")
        scaled_ready = sem("scaled_ready")
        k_ready = sem("k_ready")
        cmax_ready = sem("cmax_ready")
        shift_ready = sem("shift_ready")
        step_ready = sem("step_ready")
        alpha_ready = sem("alpha_ready")
        e_ready = sem("e_ready")
        et_ready = sem("et_ready")
        e_hi_ready = sem("e_hi_ready")
        e_lo_ready = sem("e_lo_ready")
        x_hi_ready = sem("x_hi_ready")
        x_lo_ready = sem("x_lo_ready")
        a_ready = sem("a_ready")
        a_added = sem("a_added")
        z_old_ready = sem("z_old_ready")
        z_ready = sem("z_ready")
        rz_ready = sem("rz_ready")
        a_norm = sem("a_norm")
        u_ps = sem("u_ps")
        u_ready = sem("u_ready")
        m_ps = sem("m_ps")
        m_full_ready = sem("m_full_ready")
        m_hi_ready = sem("m_hi_ready")
        m_ready = sem("m_ready")
        m_diff_ready = sem("m_diff_ready")
        bias_ps = sem("bias_ps")
        bias_ready = sem("bias_ready")
        r_ready = sem("r_ready")
        o_ready = sem("o_ready")

        halves = ((0, 0), (0, 1), (1, 0))

        def slot(p, parity):
            return NCH + DOUBLED.index(p) if parity and p in DOUBLED else p

        def image_pairs(engine, period):
            with engine.Fori(0, (B - 2) // 2) as i:
                period(i * 2 + 1, 1)
                period(i * 2 + 2, 0)

        block = ctx.enter_context(nc.Block())

        @block.sync
        def _(sp):
            sp.dma_start(x_nat[:, 0, :], x_chunks[0]).then_inc(x_loaded[0], 16)
            sp.dma_start(wqkv, w_qkv.rearrange("(j p) n -> p j n", p=P)).then_inc(w_loaded, 16)
            sp.dma_start(wo, w_out.rearrange("(j p) n -> p j n", p=P)).then_inc(w_loaded, 16)
            sp.dma_start(b_row[:], b_out.rearrange("(a n) -> a n", a=1)).then_inc(w_loaded, 16)
            for p in TURN_ORDER[1:]:
                sp.dma_start(x_nat[:, p, :], x_chunks[p]).then_inc(x_loaded[p], 16)

            def load(b, p):
                sp.wait_ge(x_lo_ready, b * NCH + (p + 1 - NCH))
                sp.dma_start(x_nat[:, p, :], x_chunks[bass.ds(b * NCH + p, 1)].rearrange(
                    "a p n -> (a p) n")).then_inc(x_loaded[p], 16)

            def store(b, p):
                sp.wait_ge(o_ready, b * NCH + (p + 1))
                sp.dma_start(out_chunks[bass.ds(b * NCH + p, 1)].rearrange("a p n -> (a p) n"),
                             o_stage[:, p % 2, :]).then_inc(stored[p % 2], 16)

            def period(b, parity, first=False, last=False):
                if not first:
                    store(b - 1, 4)
                    store(b - 1, 5)
                if not last:
                    for p in range(NCH):
                        load(b + 1, p)
                if not first:
                    for p in LATE:
                        store(b - 1, p)
                for p in range(4):
                    store(b, p)

            period(0, 0, first=True)
            image_pairs(sp, period)
            period(B - 1, 1, last=True)
            for p in range(4, NCH):
                store(B - 1, p)
            for s in stored:
                sp.wait_ge(s, 16 * B * NCH // 2)

        @block.gpsimd
        def _(pool):
            nc.gpsimd.memset(ones[:], 1.0).then_inc(consts_ready, 1)
            nc.gpsimd.memset(neg_half[:], -0.5).then_inc(consts_ready, 1)
            nc.gpsimd.memset(zero_eye[:], 0.0).then_inc(filled, 1)
            pool.wait_ge(filled, 1)
            nc.gpsimd.affine_select(out=ident, in_=ident, compare_op=ALU.not_equal, fill=1.0, base=0,
                                    pattern=[[-1, P]], channel_multiplier=1).then_inc(consts_ready, 1)
            nc.gpsimd.memset(grp[:], 1.0 / GC).then_inc(filled, 1)
            pool.wait_ge(filled, 2)
            g3 = grp[:].rearrange("p (g i) -> p g i", i=GC)
            nc.gpsimd.affine_select(out=g3, in_=g3, compare_op=ALU.is_ge, fill=0.0, base=0,
                                    pattern=[[-GC, P // GC], [0, GC]], channel_multiplier=1).then_inc(filled, 1)
            pool.wait_ge(filled, 3)
            nc.gpsimd.affine_select(out=g3, in_=g3, compare_op=ALU.is_ge, fill=0.0, base=GC - 1,
                                    pattern=[[GC, P // GC], [0, GC]], channel_multiplier=-1).then_inc(consts_ready, 1)

            def rstd_of(b):
                pool.wait_ge(var_eps_ready, b + 1)
                nc.gpsimd.tensor_tensor(rstd[:], var_eps[:], neg_half[:], ALU.pow).then_inc(rstd_ready, 1)

            def add_bias(b, p):
                pool.wait_ge(r_read, b * NCH + (p + 1))
                if p == 0:
                    pool.wait_ge(bias_ready, b + 1)
                o = o_stage[:, p % 2, :].rearrange("p (t c) -> p t c", t=TILES)
                nc.gpsimd.tensor_tensor(o, o, bias[:].unsqueeze(1).broadcast_to([P, TILES, C]),
                                        ALU.add).then_inc(o_ready, 1)

            def period(b, parity, first=False, last=False):
                if not first:
                    for p in LATE:
                        add_bias(b - 1, p)
                for p in range(4):
                    add_bias(b, p)
                if not last:
                    rstd_of(b + 1)
                add_bias(b, 4)
                add_bias(b, 5)

            rstd_of(0)
            period(0, 0, first=True)
            image_pairs(pool, period)
            period(B - 1, 1, last=True)
            for p in LATE:
                add_bias(B - 1, p)

        @block.tensor
        def _(pe):
            def turn(b, parity, n, first=False):
                p = TURN_ORDER[n]
                to = ps_turn[n % 2]
                pe.wait_ge(x_loaded[p], b * 16 + 16)
                if n >= 2:
                    pe.wait_ge(xt_lo_ready, b * NCH + (n - 1))
                elif n == 1 and not first:
                    pe.wait_ge(bias_ready, b)
                elif n == 0 and not first:
                    pe.wait_ge(e_lo_ready, b * (2 * NCH))
                for c in range(CB):
                    for t in range(TILES):
                        last = nc.tensor.transpose(to[:, c, t * P:(t + 1) * P],
                                                   x_nat[:, p, t * C + c * P:t * C + (c + 1) * P], ident)
                last.then_inc(xt_ps_ready, 1)

            def stats(b):
                pe.wait_ge(mv_ready, b + 1)
                nc.tensor.matmul(ps_t[:, 0, 0:CB], grp[:], mv[:, :, 0], start=True, stop=True).then_inc(mean_ps, 1)
                pe.wait_ge(var2_ready, b + 1)
                nc.tensor.matmul(ps_t[:, 0, CB:2 * CB], grp[:], var2[:], start=True, stop=True).then_inc(var_ps, 1)

            def keys(b, parity, j):
                for d in range(CB):
                    n = 0
                    for ws, xs in halves:
                        if j == 0 and d == 0 and ws == 1:
                            pe.wait_ge(wk_ready, b + 1)
                        for c in range(CB):
                            last = nc.tensor.matmul(ps_k[:, j % 2, d, :],
                                                    (wk_hi, wk_lo)[ws][:, c, d * P:(d + 1) * P],
                                                    (xt_hi, xt_lo)[xs][:, slot(j, parity), c, :],
                                                    start=(n == 0), stop=(n == 3 * CB - 1))
                            n += 1
                last.then_inc(k_ready, 1)

            def turn_e(b, j, h):
                for u in range(2):
                    t = 2 * h + u
                    for d in range(CB):
                        last = nc.tensor.transpose(ps_t[:, h, u * C + d * P:u * C + (d + 1) * P],
                                                   e_dn[:, j % 2, d, t * P:(t + 1) * P], ident)
                last.then_inc(et_ready, 1)

            def gather(b, j, h):
                pe.wait_ge(e_lo_ready, b * (2 * NCH) + (2 * j + h + 1))
                if h == 0:
                    pe.wait_ge(x_lo_ready, b * NCH + (j + 1))
                    if j >= 2:
                        pe.wait_ge(a_added, b * NCH + (j - 1))
                for u in range(2):
                    t = 2 * h + u
                    for d in range(CB):
                        for n, (es, xs) in enumerate(halves):
                            first = h == 0 and u == 0 and d == 0 and n == 0
                            final = h == 1 and u == 1 and n == 2
                            last = nc.tensor.matmul(ps_a[:, j % 2, d * C:(d + 1) * C],
                                                    (e_hi, e_lo)[es][:, h, u * C + d * P:u * C + (d + 1) * P],
                                                    (x_hi, x_lo)[xs][:, j % 2, t * C:(t + 1) * C],
                                                    start=first, stop=final, skip_group_check=True)
                if h == 1:
                    last.then_inc(a_ready, 1)

            def attend(b, parity, first):
                pe.wait_ge(wk_hi_ready, b + 1)
                pe.wait_ge(xt_lo_ready, b * NCH + NCH)
                if not first:
                    pe.wait_ge(r_read, b * NCH - 3)
                keys(b, parity, 0)
                for j in range(NCH):
                    if j + 1 < NCH:
                        if j >= 1:
                            pe.wait_ge(e_ready, b * NCH + j)
                        elif not first:
                            pe.wait_ge(r_read, b * NCH - 2)
                        keys(b, parity, j + 1)
                    pe.wait_ge(e_ready, b * NCH + (j + 1))
                    if j >= 1:
                        pe.wait_ge(e_lo_ready, b * (2 * NCH) + (2 * j - 1))
                    turn_e(b, j, 0)
                    if j >= 1:
                        gather(b, j - 1, 1)
                    turn_e(b, j, 1)
                    gather(b, j, 0)
                gather(b, NCH - 1, 1)

            def combine_u(b):
                pe.wait_ge(a_norm, b + 1)
                for c in range(CB):
                    for d in range(CB):
                        last = nc.tensor.matmul(ps_a[:, 0, c * C:(c + 1) * C], acc[:, d, c * P:(c + 1) * P],
                                                wq_t[:, d, :], start=(c == 0 and d == 0), stop=(d == CB - 1),
                                                skip_group_check=True)
                last.then_inc(u_ps, 1)

            def combine_m(b):
                pe.wait_ge(u_ready, b + 1)
                pe.wait_ge(scaled_ready, b + 1)
                for i in range(CB):
                    for c in range(CB):
                        last = nc.tensor.matmul(ps_a[:, 1, i * C:(i + 1) * C], u_sb[:, c, i * P:(i + 1) * P],
                                                wvo_r[:, c, :], start=(i == 0 and c == 0), stop=(c == CB - 1),
                                                skip_group_check=True)
                last.then_inc(m_ps, 1)

            def bias_row(b):
                pe.wait_ge(m_diff_ready, b + 1)
                for c in range(CB):
                    last = nc.tensor.matmul(ps_a[:, 0, 0:C], neg_mean_bc[:, c, :], m_diff[:, c, :],
                                            start=(c == 0), stop=(c == CB - 1))
                last.then_inc(bias_ps, 1)

            def emit(b, parity, p, first=False):
                if p not in LATE and not (first and p < 2):
                    pe.wait_ge(r_read, b * NCH + (p - 1))
                if p == 0:
                    pe.wait_ge(m_hi_ready, b + 1)
                for t in range(TILES):
                    n = 0
                    for ms, xs in halves:
                        if p == 0 and t == 0 and ms == 1:
                            pe.wait_ge(m_ready, b + 1)
                        for c in range(CB):
                            last = nc.tensor.matmul(ps_k[:, p % 2, t // 2, (t % 2) * C:(t % 2 + 1) * C],
                                                    (xt_hi, xt_lo)[xs][:, slot(p, parity), c, t * P:(t + 1) * P],
                                                    (m_hi, m_lo)[ms][:, c, :],
                                                    start=(t % 2 == 0 and n == 0), stop=(n == 3 * CB - 1),
                                                    skip_group_check=True)
                            n += 1
                last.then_inc(r_ready, 1)

            pe.wait_ge(consts_ready, 4)
            pe.wait_ge(w_loaded, 48)
            for i, first_col in enumerate((0, 2 * C)):
                for n in range(CB):
                    for c in range(CB):
                        last = nc.tensor.transpose(
                            ps_k[:, i, n, c * P:(c + 1) * P],
                            wqkv[:, c, first_col + n * P:first_col + (n + 1) * P], ident)
                last.then_inc(setup_ps, 1)
            turn(0, 0, 0, first=True)
            turn(0, 0, 1, first=True)
            pe.wait_ge(setup_sb, 2)
            for c in range(CB):
                for e in range(CB):
                    last = nc.tensor.matmul(ps_k[:, 0, c, 0:C], wv_t[:, e, c * P:(c + 1) * P], wo[:, e, :],
                                            start=(e == 0), stop=(e == CB - 1))
            last.then_inc(setup_ps, 1)
            for d in range(CB):
                nc.tensor.matmul(ps_k[:, 1, 0, 0:C], ones[:], wq_t[:, d, :], start=(d == 0), stop=(d == CB - 1))
            nc.tensor.matmul(ps_k[:, 1, 1, 0:C], ones[0:1, :], b_row[:], start=True, stop=True).then_inc(setup_ps, 1)

            for n in range(2, NCH):
                turn(0, 0, n, first=True)
            stats(0)
            pe.wait_ge(setup_sb, 6)

            def period(b, parity, first=False, last=False):
                def next_turn(n):
                    if not last:
                        turn(b + 1, 1 - parity, n)

                attend(b, parity, first)
                next_turn(0)
                if not first:
                    emit(b - 1, 1 - parity, 6)
                combine_u(b)
                if not first:
                    emit(b - 1, 1 - parity, 7)
                combine_m(b)
                emit(b, parity, 0, first)
                bias_row(b)
                next_turn(1)
                emit(b, parity, 1, first)
                next_turn(2)
                next_turn(3)
                emit(b, parity, 2)
                next_turn(4)
                emit(b, parity, 3)
                next_turn(5)
                next_turn(6)
                next_turn(7)
                emit(b, parity, 4)
                emit(b, parity, 5)
                if not last:
                    stats(b + 1)

            period(0, 0, first=True)
            image_pairs(pe, period)
            period(B - 1, 1, last=True)
            pe.wait_ge(r_read, B * NCH - 3)
            emit(B - 1, 1, 6)
            pe.wait_ge(r_read, B * NCH - 2)
            emit(B - 1, 1, 7)

        @block.scalar
        def _(act):
            def turn(b, parity, n):
                act.wait_ge(xt_ps_ready, b * NCH + (n + 1))
                nc.scalar.activation(xt_hi[:, slot(TURN_ORDER[n], parity), :, :], ps_turn[n % 2][:],
                                     ACT.Copy).then_inc(xt_hi_ready, 1)

            def e_high(b, j, h):
                act.wait_ge(et_ready, b * (2 * NCH) + (2 * j + h + 1))
                nc.scalar.activation(e_hi[:, h, :], ps_t[:, h, :], ACT.Copy).then_inc(e_hi_ready, 1)

            def x_high(b, j):
                if j >= 2:
                    act.wait_ge(a_ready, b * NCH + (j - 1))
                nc.scalar.activation(x_hi[:, j % 2, :], x_nat[:, j, :], ACT.Copy).then_inc(x_hi_ready, 1)

            def exps(b, j):
                act.wait_ge(shift_ready, b * NCH + (j + 1))
                for d in range(CB):
                    last = nc.scalar.activation(e_dn[:, j % 2, d, :], ps_k[:, j % 2, d, :], ACT.Exp,
                                                bias=neg_max[:, j, d:d + 1], accum_out=e_sum[:, j, d:d + 1])
                last.then_inc(e_ready, 1)
                if j >= 1:
                    act.wait_ge(step_ready, b * (NCH - 1) + j)
                    nc.scalar.activation(alpha[:, j, :], max_step[:, j, :], ACT.Exp).then_inc(alpha_ready, 1)

            def attend(b):
                for p in range(NCH):
                    act.wait_ge(x_loaded[p], b * 16 + 16)
                for j in range(NCH):
                    if j >= 1:
                        e_high(b, j - 1, 0)
                        e_high(b, j - 1, 1)
                    x_high(b, j)
                    exps(b, j)
                e_high(b, NCH - 1, 0)
                e_high(b, NCH - 1, 1)

            def emit(b, p, first=False):
                act.wait_ge(r_ready, b * NCH + (p + 1))
                if not (first and p < 2):
                    act.wait_ge(stored[p % 2], b * (16 * NCH // 2) + 16 * (p // 2))
                nc.scalar.activation(o_stage[:, p % 2, :], ps_k[:, p % 2, :, :].rearrange("p g n -> p (g n)"),
                                     ACT.Copy).then_inc(r_read, 1)

            def period(b, parity, first=False, last=False):
                def next_turn(n):
                    if not last:
                        turn(b + 1, 1 - parity, n)

                attend(b)
                next_turn(0)
                if not first:
                    for p in LATE:
                        emit(b - 1, p)
                emit(b, 0, first)
                next_turn(1)
                emit(b, 1, first)
                next_turn(2)
                next_turn(3)
                emit(b, 2)
                next_turn(4)
                emit(b, 3)
                next_turn(5)
                next_turn(6)
                next_turn(7)
                emit(b, 4)
                emit(b, 5)

            for n in range(NCH):
                turn(0, 0, n)
            period(0, 0, first=True)
            image_pairs(act, period)
            period(B - 1, 1, last=True)
            for p in LATE:
                emit(B - 1, p)

        @block.vector
        def _(dve):
            def turn_stats(b, n):
                dve.wait_ge(xt_hi_ready, b * NCH + (n + 1))
                for c in range(CB):
                    last = nc.vector.bn_stats(bn[:, c, n, :], ps_turn[n % 2][:, c, :])
                if n == NCH - 1:
                    last.then_inc(bn_ready, 1)

            def turn_low(b, parity, n):
                s = slot(TURN_ORDER[n], parity)
                nc.vector.tensor_tensor(xt_lo[:, s, :, :], ps_turn[n % 2][:], xt_hi[:, s, :, :].bitcast(F32),
                                        ALU.subtract).then_inc(xt_lo_ready, 1)

            def turn(b, parity, n):
                turn_stats(b, n)
                turn_low(b, parity, n)

            def stats(b, parity):
                turn_stats(b, NCH - 1)
                dve.wait_ge(bn_ready, b + 1)
                nc.vector.memset(wait_holder[:], 0.0)
                for c in range(CB):
                    last = nc.vector.bn_aggr(mv[:, c, :], bn[:, c, :, :].rearrange("p k s -> p (k s)"))
                last.then_inc(mv_ready, 1)
                dve.wait_ge(mean_ps, b + 1)
                nc.vector.tensor_tensor(dev[:], mv[:, :, 0], ps_t[:, 0, 0:CB], ALU.subtract)
                nc.vector.tensor_scalar(neg_mean[:], ps_t[:, 0, 0:CB], -1.0, None, ALU.mult).then_inc(mean_read, 1)
                dve.wait_ge(mean_read, b + 1)
                nc.vector.tensor_tensor(dev2[:], dev[:], dev[:], ALU.mult).then_inc(dev2_ready, 1)
                dve.wait_ge(dev2_ready, b + 1)
                nc.vector.tensor_tensor(var2[:], dev2[:], mv[:, :, 1], ALU.add).then_inc(var2_ready, 1)
                dve.wait_ge(var_ps, b + 1)
                nc.vector.tensor_scalar(var_eps[:], ps_t[:, 0, CB:2 * CB], EPS, None,
                                        ALU.add).then_inc(var_eps_ready, 1)
                turn_low(b, parity, NCH - 1)
                dve.wait_ge(rstd_ready, b + 1)
                for c in range(CB):
                    last = nc.vector.tensor_scalar(wk_hi[:, c, :], wk[:, c, :], rstd[:, c:c + 1], None, ALU.mult)
                last.then_inc(wk_hi_ready, 1)
                dve.wait_ge(wk_hi_ready, b + 1)
                for c in range(CB):
                    last = nc.vector.scalar_tensor_tensor(out=wk_lo[:, c, :], in0=wk[:, c, :],
                                                          scalar=rstd[:, c:c + 1], in1=wk_hi[:, c, :].bitcast(F32),
                                                          op0=ALU.mult, op1=ALU.subtract)
                last.then_inc(wk_ready, 1)
                for c in range(CB):
                    nc.vector.tensor_scalar(wvo_r[:, c, :], wvo[:, c, :], rstd[:, c:c + 1], None, ALU.mult)
                    last = nc.vector.tensor_scalar(neg_mean_bc[:, c, :], ones[:], neg_mean[:, c:c + 1], None,
                                                   ALU.mult)
                last.then_inc(scaled_ready, 1)

            def chunk_max(b, j):
                dve.wait_ge(k_ready, b * NCH + (j + 1))
                nc.vector.tensor_reduce(cmax[:, j, :], ps_k[:, j % 2, :, :], AX_X, ALU.max).then_inc(cmax_ready, 1)

            def shift(b, j):
                dve.wait_ge(cmax_ready, b * NCH + (j + 1))
                if j == 0:
                    nc.vector.tensor_scalar(neg_max[:, 0, :], cmax[:, 0, :], -1.0, None,
                                            ALU.mult).then_inc(shift_ready, 1)
                    return
                nc.vector.scalar_tensor_tensor(out=neg_max[:, j, :], in0=cmax[:, j, :], scalar=-1.0,
                                               in1=neg_max[:, j - 1, :], op0=ALU.mult,
                                               op1=ALU.min).then_inc(shift_ready, 1)
                dve.wait_ge(shift_ready, b * NCH + (j + 1))
                nc.vector.tensor_tensor(max_step[:, j, :], neg_max[:, j, :], neg_max[:, j - 1, :],
                                        ALU.subtract).then_inc(step_ready, 1)

            def e_low(b, j, h):
                dve.wait_ge(e_hi_ready, b * (2 * NCH) + (2 * j + h + 1))
                nc.vector.tensor_tensor(e_lo[:, h, :], ps_t[:, h, :], e_hi[:, h, :].bitcast(F32),
                                        ALU.subtract).then_inc(e_lo_ready, 1)

            def add_a(b, j):
                dve.wait_ge(a_ready, b * NCH + (j + 1))
                if j == 0:
                    nc.vector.tensor_copy(z[:], e_sum[:, 0, :]).then_inc(z_ready, 1)
                    nc.vector.tensor_copy(acc[:], ps_a[:, 0, :].rearrange("p (d c) -> p d c", d=CB)).then_inc(
                        a_added, 1)
                    return
                dve.wait_ge(alpha_ready, b * (NCH - 1) + j)
                dve.wait_ge(a_added, b * NCH + j)
                dve.wait_ge(z_ready, b * NCH + j)
                nc.vector.tensor_tensor(z_old[:, j, :], z[:], alpha[:, j, :], ALU.mult).then_inc(z_old_ready, 1)
                for d in range(CB):
                    last = nc.vector.scalar_tensor_tensor(out=acc[:, d, :], in0=acc[:, d, :],
                                                          scalar=alpha[:, j, d:d + 1],
                                                          in1=ps_a[:, j % 2, d * C:(d + 1) * C],
                                                          op0=ALU.mult, op1=ALU.add)
                last.then_inc(a_added, 1)
                dve.wait_ge(z_old_ready, b * (NCH - 1) + j)
                nc.vector.tensor_tensor(z[:], z_old[:, j, :], e_sum[:, j, :], ALU.add).then_inc(z_ready, 1)

            def x_low(b, j):
                dve.wait_ge(x_hi_ready, b * NCH + (j + 1))
                nc.vector.tensor_tensor(x_lo[:, j % 2, :], x_nat[:, j, :], x_hi[:, j % 2, :].bitcast(F32),
                                        ALU.subtract).then_inc(x_lo_ready, 1)

            def attend(b):
                for j in range(NCH):
                    chunk_max(b, j)
                    if j >= 1:
                        e_low(b, j - 1, 0)
                    shift(b, j)
                    if j >= 1:
                        e_low(b, j - 1, 1)
                    if j >= 2:
                        add_a(b, j - 2)
                    x_low(b, j)
                e_low(b, NCH - 1, 0)
                e_low(b, NCH - 1, 1)
                add_a(b, NCH - 2)
                add_a(b, NCH - 1)

            def normalise(b):
                dve.wait_ge(z_ready, b * NCH + NCH)
                nc.vector.reciprocal(rz[:], z[:]).then_inc(rz_ready, 1)
                dve.wait_ge(rz_ready, b + 1)
                for d in range(CB):
                    last = nc.vector.tensor_scalar(acc[:, d, :], acc[:, d, :], rz[:, d:d + 1], None, ALU.mult)
                last.then_inc(a_norm, 1)

            def take_u(b):
                dve.wait_ge(u_ps, b + 1)
                for c in range(CB):
                    last = nc.vector.scalar_tensor_tensor(out=u_sb[:, c, :], in0=wq_sum[:],
                                                          scalar=neg_mean[:, c:c + 1],
                                                          in1=ps_a[:, 0, c * C:(c + 1) * C],
                                                          op0=ALU.mult, op1=ALU.add)
                last.then_inc(u_ready, 1)

            def take_m(b):
                dve.wait_ge(m_ps, b + 1)
                for i in range(CB):
                    last = nc.vector.scalar_tensor_tensor(out=m_full[:, i, :], in0=ps_a[:, 1, i * C:(i + 1) * C],
                                                          scalar=rstd[:, i:i + 1], in1=eye[i],
                                                          op0=ALU.mult, op1=ALU.add)
                last.then_inc(m_full_ready, 1)
                dve.wait_ge(m_full_ready, b + 1)
                nc.vector.tensor_copy(m_hi[:], m_full[:]).then_inc(m_hi_ready, 1)
                dve.wait_ge(m_hi_ready, b + 1)
                nc.vector.tensor_tensor(m_lo[:], m_full[:], m_hi[:].bitcast(F32), ALU.subtract).then_inc(m_ready, 1)
                for i in range(CB):
                    last = nc.vector.tensor_tensor(m_diff[:, i, :], m_full[:, i, :], eye[i], ALU.subtract)
                last.then_inc(m_diff_ready, 1)

            def bias_row(b, first):
                dve.wait_ge(bias_ps, b + 1)
                if not first:
                    dve.wait_ge(o_ready, b * NCH)
                nc.vector.tensor_tensor(bias[:], ps_a[:, 0, 0:C], b_tile[:], ALU.add).then_inc(bias_ready, 1)

            for i, to in enumerate((wq_t, wv_t)):
                dve.wait_ge(setup_ps, i + 1)
                nc.vector.tensor_copy(to[:], ps_k[:, i, :, 0:C]).then_inc(setup_sb, 1)
            nc.vector.tensor_copy(wk[:], wqkv[:, :, C:2 * C]).then_inc(setup_sb, 1)
            dve.wait_ge(setup_ps, 3)
            nc.vector.tensor_copy(wvo[:], ps_k[:, 0, :, 0:C]).then_inc(setup_sb, 1)
            dve.wait_ge(setup_ps, 4)
            nc.vector.tensor_copy(wq_sum[:], ps_k[:, 1, 0, 0:C]).then_inc(setup_sb, 1)
            nc.vector.tensor_copy(b_tile[:], ps_k[:, 1, 1, 0:C]).then_inc(setup_sb, 1)
            dve.wait_ge(setup_sb, 6)

            for n in range(NCH - 1):
                turn(0, 0, n)
            stats(0, 0)

            def period(b, parity, first=False, last=False):
                attend(b)
                normalise(b)
                if not last:
                    turn_stats(b + 1, 0)
                take_u(b)
                if not last:
                    turn_low(b + 1, 1 - parity, 0)
                take_m(b)
                bias_row(b, first)
                if not last:
                    for n in range(1, NCH - 1):
                        turn(b + 1, 1 - parity, n)
                    stats(b + 1, 1 - parity)

            period(0, 0, first=True)
            image_pairs(dve, period)
            period(B - 1, 1, last=True)


_INS = ["x", "L0_conv_W_qkv", "L0_conv_W_out", "L0_conv_b_out"]


def kernel(**inputs):
    import numpy as np
    import concourse.bacc as bacc
    from concourse.bass_utils import run_bass_kernel_spmd

    nc = bacc.Bacc("TRN2", target_bir_lowering=False, num_devices=1)
    arrays, args = {}, []
    for name in _INS:
        a = np.ascontiguousarray(inputs[name])
        arrays[f"in_{name}_dram"] = a
        args.append(nc.dram_tensor(f"in_{name}_dram", a.shape, mybir.dt.from_np(a.dtype), kind="ExternalInput").ap())
    o = nc.dram_tensor("out_0_dram", inputs["x"].shape, F32, kind="ExternalOutput").ap()
    build(nc, *args, o)
    r = run_bass_kernel_spmd(nc, [arrays], core_ids=[0])
    return r.results[0]["out_0_dram"]
```

```python
from contextlib import ExitStack

import concourse.bass as bass
from concourse import mybir

ALU = mybir.AluOpType
ACT = mybir.ActivationFunctionType
AX_X = mybir.AxisListType.X
F32 = mybir.dt.float32
F32R = mybir.dt.float32r

P = 128
GROUPS = 32
EPS = 1e-5
TILES = 4
CH = TILES * P
LATE = (6, 7)
TURN_ORDER = (4, 5, 6, 7, 0, 3, 1, 2)
DOUBLED = (3, 4, 5, 6, 7)


def build(nc: bass.Bass, x: bass.AP, w_qkv: bass.AP, w_out: bass.AP, b_out: bass.AP, out: bass.AP):
    B, H, W, C = x.shape
    NCH = H * W // CH
    CB = C // P
    GC = C // GROUPS
    assert CB == 2 and NCH == 8 and P % GC == 0

    x_chunks = x.rearrange("b h w c -> (b h w) c").rearrange("(g p t) c -> g p (t c)", p=P, t=TILES)
    out_chunks = out.rearrange("b h w c -> (b h w) c").rearrange("(g p t) c -> g p (t c)", p=P, t=TILES)

    with ExitStack() as ctx:
        def sb(name, shape, dt=F32):
            return ctx.enter_context(nc.sbuf_tensor(name, shape, dt))

        def psum(name, shape):
            return ctx.enter_context(nc.psum_tensor(name, shape, F32))

        def sem(name):
            return ctx.enter_context(nc.semaphore(name))

        x_nat = sb("x_nat", [P, NCH, TILES * C])
        xt_hi = sb("xt_hi", [P, NCH + len(DOUBLED), CB, CH], F32R)
        with nc.sbuf_tensor("x0t", [P, NCH, CB, CH], F32) as x0t:
            pass
        xt_lo = sb("xt_lo", [P, NCH + len(DOUBLED), CB, CH], F32R)
        x_hi = sb("x_hi", [P, 2, TILES * C], F32R)
        x_lo = sb("x_lo", [P, 2, TILES * C], F32R)
        e_dn = sb("e_dn", [P, 2, CB, CH])
        e_hi = sb("e_hi", [P, 2, 2 * C], F32R)
        e_lo = sb("e_lo", [P, 2, 2 * C], F32R)
        o_stage = sb("o_stage", [P, 2, TILES * C])
        w_stage = e_dn[:].rearrange("p a d n -> p (a d n)")
        wqkv = w_stage[:, 0:CB * 3 * C].rearrange("p (j n) -> p j n", j=CB)
        wo = w_stage[:, CB * 3 * C:CB * 4 * C].rearrange("p (j n) -> p j n", j=CB)
        wk = sb("wk", [P, CB, C])
        wq_t = sb("wq_t", [P, CB, C])
        wvo = sb("wvo", [P, CB, C])
        wq_sum = sb("wq_sum", [P, C])
        b_row = sb("b_row", [1, C])
        b_tile = sb("b_tile", [P, C])
        ones = sb("ones", [P, P])
        zero_eye = sb("zero_eye", [P, 3 * P])
        ident = zero_eye[:, P:2 * P]
        eye = [zero_eye[:, P:3 * P], zero_eye[:, 0:2 * P]]
        grp = sb("grp", [P, P])
        neg_half = sb("neg_half", [P, CB])
        bn = sb("bn", [P, CB, NCH, 6])
        mv = sb("mv", [P, CB, 2])
        wait_holder = sb("wait_holder", [P, 1])
        dev = sb("dev", [P, CB])
        var2 = sb("var2", [P, CB])
        neg_mean = sb("neg_mean", [P, CB])
        var_eps = sb("var_eps", [P, CB])
        rstd = sb("rstd", [P, CB])
        neg_mean_bc = sb("neg_mean_bc", [P, CB, P])
        wk_hi = sb("wk_hi", [P, CB, C], F32R)
        wk_lo = sb("wk_lo", [P, CB, C], F32R)
        wvo_r = sb("wvo_r", [P, CB, C])
        cmax = sb("cmax", [P, NCH, CB])
        neg_max = sb("neg_max", [P, NCH, CB])
        max_step = sb("max_step", [P, NCH, CB])
        alpha = sb("alpha", [P, NCH, CB])
        e_sum = sb("e_sum", [P, NCH, CB])
        z = sb("z", [P, CB])
        z_old = sb("z_old", [P, NCH, CB])
        rz = sb("rz", [P, CB])
        alpha_rz = sb("alpha_rz", [P, CB])
        acc = sb("acc", [P, CB, C])
        u_sb = sb("u_sb", [P, CB, C])
        m_full = acc
        m_hi = sb("m_hi", [P, CB, C], F32R)
        m_lo = sb("m_lo", [P, CB, C], F32R)
        m_diff = u_sb
        wv_t = u_sb
        bias = sb("bias", [P, C])

        ps_k = psum("ps_k", [P, 2, CB, CH])
        ps_t = psum("ps_t", [P, 2, 2 * C])
        ps_a = psum("ps_a", [P, 2, CB * C])

        def ps_keys(j):
            return ps_k[:, (j + 1) % 2, :, :]

        def ps_result(p, last_image=False):
            return ps_k[:, (p if p < 5 or last_image else p + 1) % 2, :, :]

        def ps_turn_0(p):
            return (ps_a, ps_t)[p % 2]

        def ps_turn(n):
            if n == 0:
                return ps_keys(NCH - 1)
            return (ps_t, ps_t, ps_a, ps_t, ps_a, ps_t, ps_a)[n - 1]

        w_loaded = sem("w_loaded")
        x_loaded = [sem(f"x_loaded{p}") for p in range(NCH)]
        stored = [sem(f"stored{i}") for i in range(2)]
        filled = sem("filled")
        consts_ready = sem("consts_ready")
        bn_ready = sem("bn_ready")
        r_read = sem("r_read")
        setup_ps = sem("setup_ps")
        setup_sb = sem("setup_sb")
        x0t_ps = sem("x0t_ps")
        x0t_full = sem("x0t_full")
        xt_ps_ready = sem("xt_ps_ready")
        xt_hi_ready = sem("xt_hi_ready")
        xt_lo_ready = sem("xt_lo_ready")
        mv_ready = sem("mv_ready")
        mean_ps = sem("mean_ps")
        mean_read = sem("mean_read")
        var2_ready = sem("var2_ready")
        var_ps = sem("var_ps")
        var_eps_ready = sem("var_eps_ready")
        rstd_ready = sem("rstd_ready")
        wk_hi_ready = sem("wk_hi_ready")
        wk_ready = sem("wk_ready")
        scaled_ready = sem("scaled_ready")
        k0_ready = sem("k0_ready")
        k_ready = sem("k_ready")
        cmax_ready = sem("cmax_ready")
        shift_ready = sem("shift_ready")
        step_ready = sem("step_ready")
        alpha_ready = sem("alpha_ready")
        e_ready = sem("e_ready")
        et_ready = sem("et_ready")
        e_hi_ready = sem("e_hi_ready")
        e_lo_ready = sem("e_lo_ready")
        x_hi_ready = sem("x_hi_ready")
        x_lo_ready = sem("x_lo_ready")
        a_ready = sem("a_ready")
        a_added = sem("a_added")
        z_old_ready = sem("z_old_ready")
        z_ready = sem("z_ready")
        rz_ready = sem("rz_ready")
        alpha_rz_ready = sem("alpha_rz_ready")
        a_scaled = sem("a_scaled")
        a_norm = sem("a_norm")
        u_ps = sem("u_ps")
        u_ready = sem("u_ready")
        m_ps = sem("m_ps")
        m_full_ready = sem("m_full_ready")
        m_hi_ready = sem("m_hi_ready")
        m_ready = sem("m_ready")
        m_diff_ready = sem("m_diff_ready")
        bias_ps = sem("bias_ps")
        bias_ready = sem("bias_ready")
        r5_half_read = sem("r5_half_read")
        r_ready = sem("r_ready")
        o_ready = sem("o_ready")

        halves = ((0, 0), (0, 1), (1, 0))

        def slot(p, parity):
            return NCH + DOUBLED.index(p) if parity and p in DOUBLED else p

        def image_pairs(engine, period):
            with engine.Fori(0, (B - 2) // 2) as i:
                period(i * 2 + 1, 1)
                period(i * 2 + 2, 0)

        block = ctx.enter_context(nc.Block())

        @block.sync
        def _(sp):
            for p in range(NCH):
                sp.dma_start(x_nat[:, p, :], x_chunks[p]).then_inc(x_loaded[p], 16)
            sp.dma_start(wqkv, w_qkv.rearrange("(j p) n -> p j n", p=P)).then_inc(w_loaded, 16)
            sp.dma_start(wo, w_out.rearrange("(j p) n -> p j n", p=P)).then_inc(w_loaded, 16)
            sp.dma_start(b_row[:], b_out.rearrange("(a n) -> a n", a=1)).then_inc(w_loaded, 16)

            def load(b, p):
                sp.wait_ge(x_lo_ready, b * NCH + (p + 1 - NCH))
                sp.dma_start(x_nat[:, p, :], x_chunks[bass.ds(b * NCH + p, 1)].rearrange(
                    "a p n -> (a p) n")).then_inc(x_loaded[p], 16)

            def store(b, p):
                sp.wait_ge(o_ready, b * NCH + (p + 1))
                sp.dma_start(out_chunks[bass.ds(b * NCH + p, 1)].rearrange("a p n -> (a p) n"),
                             o_stage[:, p % 2, :]).then_inc(stored[p % 2], 16)

            def period(b, parity, first=False, last=False):
                if not first:
                    for p in (3, 4, 5):
                        store(b - 1, p)
                if not last:
                    for p in range(NCH):
                        load(b + 1, p)
                if not first:
                    for p in LATE:
                        store(b - 1, p)
                for p in range(3):
                    store(b, p)

            period(0, 0, first=True)
            image_pairs(sp, period)
            period(B - 1, 1, last=True)
            for p in range(3, NCH):
                store(B - 1, p)
            for s in stored:
                sp.wait_ge(s, 16 * B * NCH // 2)

        @block.gpsimd
        def _(pool):
            nc.gpsimd.memset(ones[:], 1.0).then_inc(consts_ready, 1)
            nc.gpsimd.memset(neg_half[:], -0.5).then_inc(consts_ready, 1)
            nc.gpsimd.memset(zero_eye[:], 0.0).then_inc(filled, 1)
            pool.wait_ge(filled, 1)
            nc.gpsimd.affine_select(out=ident, in_=ident, compare_op=ALU.not_equal, fill=1.0, base=0,
                                    pattern=[[-1, P]], channel_multiplier=1).then_inc(consts_ready, 1)
            nc.gpsimd.memset(grp[:], 1.0 / GC).then_inc(filled, 1)
            pool.wait_ge(filled, 2)
            g3 = grp[:].rearrange("p (g i) -> p g i", i=GC)
            nc.gpsimd.affine_select(out=g3, in_=g3, compare_op=ALU.is_ge, fill=0.0, base=0,
                                    pattern=[[-GC, P // GC], [0, GC]], channel_multiplier=1).then_inc(filled, 1)
            pool.wait_ge(filled, 3)
            nc.gpsimd.affine_select(out=g3, in_=g3, compare_op=ALU.is_ge, fill=0.0, base=GC - 1,
                                    pattern=[[GC, P // GC], [0, GC]], channel_multiplier=-1).then_inc(consts_ready, 1)

            def rstd_of(b):
                pool.wait_ge(var_eps_ready, b + 1)
                nc.gpsimd.tensor_tensor(rstd[:], var_eps[:], neg_half[:], ALU.pow).then_inc(rstd_ready, 1)

            def add_bias(b, p):
                pool.wait_ge(r_read, b * NCH + (p + 1))
                if p == 0:
                    pool.wait_ge(bias_ready, b + 1)
                o = o_stage[:, p % 2, :].rearrange("p (t c) -> p t c", t=TILES)
                nc.gpsimd.tensor_tensor(o, o, bias[:].unsqueeze(1).broadcast_to([P, TILES, C]),
                                        ALU.add).then_inc(o_ready, 1)

            def take_diff(b):
                pool.wait_ge(m_full_ready, b + 1)
                for i in range(CB):
                    last = nc.gpsimd.tensor_tensor(m_diff[:, i, :], m_full[:, i, :], eye[i], ALU.subtract)
                last.then_inc(m_diff_ready, 1)

            def period(b, parity, first=False, last=False):
                if not first:
                    for p in (5, *LATE):
                        add_bias(b - 1, p)
                take_diff(b)
                if last:
                    return
                for p in range(3):
                    add_bias(b, p)
                rstd_of(b + 1)
                add_bias(b, 3)
                add_bias(b, 4)

            rstd_of(0)
            pool.wait_ge(xt_lo_ready, 2)
            for p in range(2, NCH):
                pool.wait_ge(xt_hi_ready, p + 1)
                nc.gpsimd.tensor_tensor(xt_lo[:, p, :, :], x0t[:, p, :, :], xt_hi[:, p, :, :].bitcast(F32),
                                        ALU.subtract).then_inc(xt_lo_ready, 1)
            period(0, 0, first=True)
            image_pairs(pool, period)
            period(B - 1, 1, last=True)

        @block.tensor
        def _(pe):
            def transposes(to, p):
                for c in range(CB):
                    for t in range(TILES):
                        last = nc.tensor.transpose(to[:, c, t * P:(t + 1) * P],
                                                   x_nat[:, p, t * C + c * P:t * C + (c + 1) * P], ident)
                return last

            def turn_0(p):
                pe.wait_ge(x_loaded[p], 16)
                if p >= 2:
                    pe.wait_ge(x0t_full, p - 1)
                transposes(ps_turn_0(p), p).then_inc(x0t_ps, 1)

            def turn(b, n):
                p = TURN_ORDER[n]
                pe.wait_ge(x_loaded[p], b * 16 + 16)
                if n == 2:
                    pe.wait_ge(xt_lo_ready, b * NCH + 2)
                elif n >= 4:
                    pe.wait_ge(xt_lo_ready, b * NCH + (n - 1))
                elif n == 3:
                    pe.wait_ge(m_full_ready, b)
                transposes(ps_turn(n), p).then_inc(xt_ps_ready, 1)

            def stats_mean(b):
                pe.wait_ge(mv_ready, b + 1)
                nc.tensor.matmul(ps_t[:, 0, 0:CB], grp[:], mv[:, :, 0], start=True, stop=True).then_inc(mean_ps, 1)

            def stats_var(b):
                pe.wait_ge(var2_ready, b + 1)
                nc.tensor.matmul(ps_t[:, 1, 0:CB], grp[:], var2[:], start=True, stop=True).then_inc(var_ps, 1)

            def keys_part(parity, j, d, n, c):
                ws, xs = halves[n]
                return nc.tensor.matmul(ps_keys(j)[:, d, :], (wk_hi, wk_lo)[ws][:, c, d * P:(d + 1) * P],
                                        (xt_hi, xt_lo)[xs][:, slot(j, parity), c, :],
                                        start=(n == 0 and c == 0), stop=(n == 2 and c == CB - 1),
                                        skip_group_check=True)

            def keys_0(b, parity):
                for d in range(CB):
                    for n in (0, 1):
                        for c in range(CB):
                            if d == 0 and n == 0:
                                pe.wait_ge(wk_hi_ready, b * CB + (c + 1))
                            keys_part(parity, 0, d, n, c)
                pe.wait_ge(wk_ready, b + 1)
                for d, ready in enumerate((k0_ready, k_ready)):
                    for c in range(CB):
                        last = keys_part(parity, 0, d, 2, c)
                    last.then_inc(ready, 1)

            def keys(b, parity, j, after_5=False):
                for d in range(CB):
                    if d == 1 and after_5:
                        pe.wait_ge(r_read, b * NCH - 2)
                    for n in range(3):
                        for c in range(CB):
                            last = keys_part(parity, j, d, n, c)
                last.then_inc(k_ready, 1)

            def turn_e0(b):
                for d in range(CB):
                    pe.wait_ge(e_ready, b * (CB * NCH) + (d + 1))
                    for h in range(2):
                        for u in range(2):
                            last = nc.tensor.transpose(ps_t[:, h, u * C + d * P:u * C + (d + 1) * P],
                                                       e_dn[:, 0, d, (2 * h + u) * P:(2 * h + u + 1) * P], ident)
                        if d == CB - 1:
                            last.then_inc(et_ready, 1)

            def turn_e(b, j, h):
                for d in range(CB):
                    if h == 0:
                        pe.wait_ge(e_ready, b * (CB * NCH) + (CB * j + d + 1))
                    for u in range(2):
                        t = 2 * h + u
                        last = nc.tensor.transpose(ps_t[:, h, u * C + d * P:u * C + (d + 1) * P],
                                                   e_dn[:, j % 2, d, t * P:(t + 1) * P], ident)
                last.then_inc(et_ready, 1)

            def gather(b, j, h):
                pe.wait_ge(e_lo_ready, b * (2 * NCH) + (2 * j + h + 1))
                if h == 0:
                    pe.wait_ge(x_lo_ready, b * NCH + (j + 1))
                    if j >= 2:
                        pe.wait_ge(a_added, b * (NCH - 1) + (j - 1))
                for u in range(2):
                    t = 2 * h + u
                    for d in range(CB):
                        for n, (es, xs) in enumerate(halves):
                            first = h == 0 and u == 0 and d == 0 and n == 0
                            final = h == 1 and u == 1 and n == 2
                            last = nc.tensor.matmul(ps_a[:, j % 2, d * C:(d + 1) * C],
                                                    (e_hi, e_lo)[es][:, h, u * C + d * P:u * C + (d + 1) * P],
                                                    (x_hi, x_lo)[xs][:, j % 2, t * C:(t + 1) * C],
                                                    start=first, stop=final, skip_group_check=True)
                if h == 1:
                    last.then_inc(a_ready, 1)

            def setup_wvo():
                for c in range(CB):
                    for e in range(CB):
                        last = nc.tensor.matmul(ps_keys(0)[:, c, 0:C], wv_t[:, e, c * P:(c + 1) * P], wo[:, e, :],
                                                start=(e == 0), stop=(e == CB - 1))
                last.then_inc(setup_ps, 1)

            def setup_rows():
                for d in range(CB):
                    nc.tensor.matmul(ps_keys(6)[:, 0, 0:C], ones[:], wq_t[:, d, :],
                                     start=(d == 0), stop=(d == CB - 1))
                nc.tensor.matmul(ps_keys(6)[:, 1, 0:C], ones[0:1, :], b_row[:],
                                 start=True, stop=True).then_inc(setup_ps, 1)

            def attend(b, parity, first):
                if first:
                    pe.wait_ge(xt_lo_ready, 1)
                else:
                    pe.wait_ge(xt_lo_ready, b * NCH + (NCH - 1))
                    pe.wait_ge(r_read, b * NCH - 4)
                keys_0(b, parity)
                if not first:
                    emit(b - 1, 1 - parity, 5)
                if first:
                    pe.wait_ge(xt_lo_ready, 2)
                    keys(b, parity, 1)
                turn_e0(b)
                if first:
                    setup_wvo()
                else:
                    pe.wait_ge(r5_half_read, b)
                    keys(b, parity, 1, after_5=True)
                if not first:
                    pe.wait_ge(xt_lo_ready, b * NCH + NCH)
                gather(b, 0, 0)
                for j in range(1, NCH - 1):
                    if first:
                        if j == 1:
                            pe.wait_ge(setup_sb, 4)
                        pe.wait_ge(xt_lo_ready, j + 2)
                    keys(b, parity, j + 1)
                    pe.wait_ge(e_lo_ready, b * (2 * NCH) + (2 * j - 1))
                    turn_e(b, j, 0)
                    gather(b, j - 1, 1)
                    turn_e(b, j, 1)
                    gather(b, j, 0)

            def combine_u(b):
                for c in range(CB):
                    for d in range(CB):
                        if c == 0:
                            pe.wait_ge(a_norm, b * CB + (d + 1))
                        last = nc.tensor.matmul(ps_a[:, c, 0:C], acc[:, d, c * P:(c + 1) * P],
                                                wq_t[:, d, :], start=(d == 0), stop=(d == CB - 1))
                    last.then_inc(u_ps, 1)

            def combine_m(b):
                pe.wait_ge(scaled_ready, b + 1)
                pe.wait_ge(u_ready, b + 1)
                for i in range(CB):
                    for c in range(CB):
                        last = nc.tensor.matmul(ps_a[:, i, 0:C], u_sb[:, c, i * P:(i + 1) * P],
                                                wvo_r[:, c, :], start=(c == 0), stop=(c == CB - 1))
                    last.then_inc(m_ps, 1)

            def bias_row(b):
                pe.wait_ge(m_diff_ready, b + 1)
                for c in range(CB):
                    last = nc.tensor.matmul(ps_k[:, 1, 0, 0:C], neg_mean_bc[:, c, :], m_diff[:, c, :],
                                            start=(c == 0), stop=(c == CB - 1))
                last.then_inc(bias_ps, 1)

            def emit(b, parity, p, t0=0, t1=TILES, first=False, last_image=False):
                read = o_ready if last_image else r_read
                if p == 5 and not last_image:
                    pe.wait_ge(read, b * NCH + 5)
                elif (p in (2, 3, 4) or (p >= 5 and last_image)) and t0 == 0:
                    pe.wait_ge(read, b * NCH + (p - 1))
                elif p == 0 and not first:
                    pe.wait_ge(r_read, b * NCH)
                if p == 0:
                    pe.wait_ge(m_hi_ready, b + 1)
                if p == 1 and t0 == 0:
                    pe.wait_ge(bias_ready, b + 1)
                for t in range(t0, t1):
                    n = 0
                    for ms, xs in halves:
                        if p == 0 and t == 0 and ms == 1:
                            pe.wait_ge(m_ready, b + 1)
                        for c in range(CB):
                            last = nc.tensor.matmul(ps_result(p, last_image)[:, t // 2, (t % 2) * C:(t % 2 + 1) * C],
                                                    (xt_hi, xt_lo)[xs][:, slot(p, parity), c, t * P:(t + 1) * P],
                                                    (m_hi, m_lo)[ms][:, c, :],
                                                    start=(t % 2 == 0 and n == 0), stop=(n == 3 * CB - 1),
                                                    skip_group_check=True)
                            n += 1
                if t1 == TILES:
                    last.then_inc(r_ready, 1)

            pe.wait_ge(consts_ready, 4)
            for p in range(NCH):
                turn_0(p)
            pe.wait_ge(w_loaded, 48)
            for i, first_col in enumerate((0, 2 * C)):
                for n in range(CB):
                    for c in range(CB):
                        last = nc.tensor.transpose(
                            ps_k[:, i, n, c * P:(c + 1) * P],
                            wqkv[:, c, first_col + n * P:first_col + (n + 1) * P], ident)
                last.then_inc(setup_ps, 1)
            stats_mean(0)
            stats_var(0)
            pe.wait_ge(setup_sb, 3)

            def period(b, parity, first=False, last=False):
                def next_turn(n):
                    if not last:
                        turn(b + 1, n)

                def late(p, half):
                    if not first:
                        emit(b - 1, 1 - parity, p, 2 * half, 2 * half + 2)

                def early(p, t0=0, t1=TILES):
                    emit(b, parity, p, t0, t1, first, last)

                attend(b, parity, first)
                late(6, 0)
                gather(b, NCH - 2, 1)
                turn_e(b, NCH - 1, 0)
                turn_e(b, NCH - 1, 1)
                next_turn(0)
                late(6, 1)
                if first:
                    setup_rows()
                gather(b, NCH - 1, 0)
                gather(b, NCH - 1, 1)
                next_turn(1)
                if not last:
                    pe.wait_ge(xt_lo_ready, b * NCH + (NCH + 1))
                late(7, 0)
                combine_u(b)
                late(7, 1)
                combine_m(b)
                next_turn(2)
                next_turn(3)
                early(0)
                if first:
                    pe.wait_ge(setup_sb, 6)
                bias_row(b)
                next_turn(4)
                early(1, 0, 2)
                next_turn(5)
                early(1, 2, 4)
                next_turn(6)
                early(2)
                next_turn(7)
                early(3, 0, 3)
                if not last:
                    stats_mean(b + 1)
                early(3, 3, 4)
                early(4, 0, 1)
                if not last:
                    stats_var(b + 1)
                early(4, 1, 4)

            period(0, 0, first=True)
            image_pairs(pe, period)
            period(B - 1, 1, last=True)
            for p in (5, *LATE):
                emit(B - 1, 1, p, last_image=True)

        @block.scalar
        def _(act):
            def full_0(p):
                act.wait_ge(x0t_ps, p + 1)
                nc.scalar.activation(x0t[:, p, :, :], ps_turn_0(p)[:], ACT.Copy).then_inc(x0t_full, 1)

            def high_0(p):
                act.wait_ge(x0t_full, p + 1)
                nc.scalar.activation(xt_hi[:, p, :, :], x0t[:, p, :, :],
                                     ACT.Copy).then_inc(xt_hi_ready, 1)

            def turn(b, parity, n):
                if n == NCH - 1:
                    act.wait_ge(bn_ready, b + 1)
                else:
                    act.wait_ge(xt_ps_ready, (b - 1) * NCH + (n + 1))
                nc.scalar.activation(xt_hi[:, slot(TURN_ORDER[n], parity), :, :], ps_turn(n)[:],
                                     ACT.Copy).then_inc(xt_hi_ready, 1)

            def e_high(b, j, h):
                act.wait_ge(et_ready, b * (2 * NCH) + (2 * j + h + 1))
                nc.scalar.activation(e_hi[:, h, :], ps_t[:, h, :], ACT.Copy).then_inc(e_hi_ready, 1)

            def x_high(b, j):
                if j >= 2:
                    act.wait_ge(a_ready, b * NCH + (j - 1))
                nc.scalar.activation(x_hi[:, j % 2, :], x_nat[:, j, :], ACT.Copy).then_inc(x_hi_ready, 1)

            def exps(b, j):
                act.wait_ge(shift_ready, b * NCH + (j + 1))
                for d in range(CB):
                    last = nc.scalar.activation(e_dn[:, j % 2, d, :], ps_keys(j)[:, d, :], ACT.Exp,
                                                bias=neg_max[:, j, d:d + 1], accum_out=e_sum[:, j, d:d + 1])
                    last.then_inc(e_ready, 1)
                if j >= 1:
                    act.wait_ge(step_ready, b * (NCH - 1) + j)
                    nc.scalar.activation(alpha[:, j, :], max_step[:, j, :], ACT.Exp).then_inc(alpha_ready, 1)

            def attend(b, first):
                for p in range(NCH):
                    act.wait_ge(x_loaded[p], b * 16 + 16)
                for j in range(NCH):
                    if j >= 1:
                        e_high(b, j - 1, 0)
                        e_high(b, j - 1, 1)
                    if first and j == 1:
                        act.wait_ge(setup_ps, 3)
                        nc.scalar.activation(wvo[:], ps_keys(0)[:, :, 0:C], ACT.Copy).then_inc(setup_sb, 1)
                    x_high(b, j)
                    exps(b, j)
                    if j == 0 and not first:
                        emit(b - 1, 5)
                e_high(b, NCH - 1, 0)
                e_high(b, NCH - 1, 1)

            def emit(b, p, first=False):
                act.wait_ge(r_ready, b * NCH + (p + 1))
                if not (first and p < 2):
                    act.wait_ge(stored[p % 2], b * (16 * NCH // 2) + 16 * (p // 2))
                if p == 5:
                    o = o_stage[:, 1, :].rearrange("p (g n) -> p g n", g=2)
                    nc.scalar.activation(o[:, 0, :], ps_result(5)[:, 0, :], ACT.Copy).then_inc(r5_half_read, 1)
                    nc.scalar.activation(o[:, 1, :], ps_result(5)[:, 1, :], ACT.Copy).then_inc(r_read, 1)
                    return
                nc.scalar.activation(o_stage[:, p % 2, :], ps_result(p).rearrange("p g n -> p (g n)"),
                                     ACT.Copy).then_inc(r_read, 1)

            def period(b, parity, first=False, last=False):
                def next_turn(n):
                    if not last:
                        turn(b + 1, 1 - parity, n)

                attend(b, first)
                next_turn(0)
                if first:
                    act.wait_ge(setup_ps, 4)
                    nc.scalar.activation(wq_sum[:], ps_keys(6)[:, 0, 0:C], ACT.Copy).then_inc(setup_sb, 1)
                    nc.scalar.activation(b_tile[:], ps_keys(6)[:, 1, 0:C], ACT.Copy).then_inc(setup_sb, 1)
                else:
                    emit(b - 1, 6)
                next_turn(1)
                if not first:
                    emit(b - 1, 7)
                next_turn(2)
                if last:
                    return
                next_turn(3)
                emit(b, 0, first)
                next_turn(4)
                next_turn(5)
                emit(b, 1, first)
                next_turn(6)
                emit(b, 2)
                next_turn(7)
                emit(b, 3)
                emit(b, 4)

            for p in range(NCH):
                full_0(p)
                if p < 2:
                    high_0(p)
            high_0(2)
            act.wait_ge(w_loaded, 48)
            nc.scalar.activation(wk[:], wqkv[:, :, C:2 * C], ACT.Copy).then_inc(setup_sb, 1)
            for i, to in enumerate((wq_t, wv_t)):
                act.wait_ge(setup_ps, i + 1)
                nc.scalar.activation(to[:], ps_k[:, i, :, 0:C], ACT.Copy).then_inc(setup_sb, 1)
            for p in range(3, NCH):
                high_0(p)
            act.wait_ge(setup_sb, 3)

            period(0, 0, first=True)
            image_pairs(act, period)
            period(B - 1, 1, last=True)

        @block.vector
        def _(dve):
            def stats_0(p):
                dve.wait_ge(x0t_full, p + 1)
                for c in range(CB):
                    last = nc.vector.bn_stats(bn[:, c, p, :], x0t[:, p, c, :])
                if p == NCH - 1:
                    last.then_inc(bn_ready, 1)

            def low_0(p):
                dve.wait_ge(xt_hi_ready, p + 1)
                if p == 0:
                    dve.wait_ge(bn_ready, 1)
                nc.vector.tensor_tensor(xt_lo[:, p, :, :], x0t[:, p, :, :],
                                        xt_hi[:, p, :, :].bitcast(F32), ALU.subtract).then_inc(xt_lo_ready, 1)

            def turn_stats(b, n):
                if n == NCH - 1:
                    dve.wait_ge(xt_ps_ready, (b - 1) * NCH + NCH)
                else:
                    dve.wait_ge(xt_hi_ready, b * NCH + (n + 1))
                for c in range(CB):
                    last = nc.vector.bn_stats(bn[:, c, n, :], ps_turn(n)[:, c, :])
                if n == NCH - 1:
                    last.then_inc(bn_ready, 1)

            def turn_low(b, parity, n):
                s = slot(TURN_ORDER[n], parity)
                nc.vector.tensor_tensor(xt_lo[:, s, :, :], ps_turn(n)[:], xt_hi[:, s, :, :].bitcast(F32),
                                        ALU.subtract).then_inc(xt_lo_ready, 1)

            def turn(b, parity, n):
                turn_stats(b, n)
                turn_low(b, parity, n)

            def stats(b, parity, first=False):
                if first:
                    stats_0(NCH - 1)
                else:
                    turn_stats(b, NCH - 1)
                dve.wait_ge(bn_ready, b + 1)
                nc.vector.memset(wait_holder[:], 0.0)
                for c in range(CB):
                    last = nc.vector.bn_aggr(mv[:, c, :], bn[:, c, :, :].rearrange("p k s -> p (k s)"))
                last.then_inc(mv_ready, 1)
                dve.wait_ge(mean_ps, b + 1)
                nc.vector.tensor_tensor(dev[:], mv[:, :, 0], ps_t[:, 0, 0:CB], ALU.subtract)
                nc.vector.tensor_scalar(neg_mean[:], ps_t[:, 0, 0:CB], -1.0, None, ALU.mult).then_inc(mean_read, 1)
                dve.wait_ge(mean_read, b + 1)
                for c in range(CB):
                    last = nc.vector.scalar_tensor_tensor(out=var2[:, c:c + 1], in0=dev[:, c:c + 1],
                                                          scalar=dev[:, c:c + 1], in1=mv[:, c, 1:2],
                                                          op0=ALU.mult, op1=ALU.add)
                last.then_inc(var2_ready, 1)
                if first:
                    low_0(0)
                dve.wait_ge(var_ps, b + 1)
                nc.vector.tensor_scalar(var_eps[:], ps_t[:, 1, 0:CB], EPS, None,
                                        ALU.add).then_inc(var_eps_ready, 1)
                dve.wait_ge(rstd_ready, b + 1)
                for c in range(CB):
                    nc.vector.tensor_scalar(wk_hi[:, c, :], wk[:, c, :], rstd[:, c:c + 1], None,
                                            ALU.mult).then_inc(wk_hi_ready, 1)
                dve.wait_ge(wk_hi_ready, b * CB + CB)
                for c in range(CB):
                    last = nc.vector.scalar_tensor_tensor(out=wk_lo[:, c, :], in0=wk[:, c, :],
                                                          scalar=rstd[:, c:c + 1], in1=wk_hi[:, c, :].bitcast(F32),
                                                          op0=ALU.mult, op1=ALU.subtract)
                last.then_inc(wk_ready, 1)
                if first:
                    low_0(1)
                else:
                    dve.wait_ge(xt_hi_ready, b * NCH + NCH)
                    turn_low(b, parity, NCH - 1)

            def scale(b):
                for c in range(CB):
                    nc.vector.tensor_scalar(wvo_r[:, c, :], wvo[:, c, :], rstd[:, c:c + 1], None, ALU.mult)
                    last = nc.vector.tensor_scalar(neg_mean_bc[:, c, :], ones[:], neg_mean[:, c:c + 1], None,
                                                   ALU.mult)
                last.then_inc(scaled_ready, 1)

            def chunk_max(b, j):
                if j == 0:
                    dve.wait_ge(k0_ready, b + 1)
                    nc.vector.tensor_reduce(cmax[:, 0, 0:1], ps_keys(0)[:, 0, :], AX_X, ALU.max)
                    dve.wait_ge(k_ready, b * NCH + 1)
                    nc.vector.tensor_reduce(cmax[:, 0, 1:2], ps_keys(0)[:, 1, :], AX_X, ALU.max).then_inc(
                        cmax_ready, 1)
                    return
                dve.wait_ge(k_ready, b * NCH + (j + 1))
                nc.vector.tensor_reduce(cmax[:, j, :], ps_keys(j), AX_X, ALU.max).then_inc(cmax_ready, 1)

            def shift(b, j):
                dve.wait_ge(cmax_ready, b * NCH + (j + 1))
                if j == 0:
                    nc.vector.tensor_scalar(neg_max[:, 0, :], cmax[:, 0, :], -1.0, None,
                                            ALU.mult).then_inc(shift_ready, 1)
                    return
                nc.vector.scalar_tensor_tensor(out=neg_max[:, j, :], in0=cmax[:, j, :], scalar=-1.0,
                                               in1=neg_max[:, j - 1, :], op0=ALU.mult,
                                               op1=ALU.min).then_inc(shift_ready, 1)
                dve.wait_ge(shift_ready, b * NCH + (j + 1))
                nc.vector.tensor_tensor(max_step[:, j, :], neg_max[:, j, :], neg_max[:, j - 1, :],
                                        ALU.subtract).then_inc(step_ready, 1)

            def e_low(b, j, h):
                dve.wait_ge(e_hi_ready, b * (2 * NCH) + (2 * j + h + 1))
                nc.vector.tensor_tensor(e_lo[:, h, :], ps_t[:, h, :], e_hi[:, h, :].bitcast(F32),
                                        ALU.subtract).then_inc(e_lo_ready, 1)

            def add_z(b, j):
                if j == 0:
                    dve.wait_ge(e_ready, b * (CB * NCH) + CB)
                    nc.vector.tensor_copy(z[:], e_sum[:, 0, :]).then_inc(z_ready, 1)
                    return
                dve.wait_ge(alpha_ready, b * (NCH - 1) + j)
                dve.wait_ge(z_ready, b * NCH + j)
                nc.vector.tensor_tensor(z_old[:, j, :], z[:], alpha[:, j, :], ALU.mult).then_inc(z_old_ready, 1)
                dve.wait_ge(z_old_ready, b * (NCH - 1) + j)
                nc.vector.tensor_tensor(z[:], z_old[:, j, :], e_sum[:, j, :], ALU.add).then_inc(z_ready, 1)

            def add_a(b, j):
                add_z(b, j)
                dve.wait_ge(a_ready, b * NCH + (j + 1))
                if j == 0:
                    nc.vector.tensor_copy(acc[:], ps_a[:, 0, :].rearrange("p (d c) -> p d c", d=CB)).then_inc(
                        a_added, 1)
                    return
                dve.wait_ge(a_added, b * (NCH - 1) + j)
                for d in range(CB):
                    last = nc.vector.scalar_tensor_tensor(out=acc[:, d, :], in0=acc[:, d, :],
                                                          scalar=alpha[:, j, d:d + 1],
                                                          in1=ps_a[:, j % 2, d * C:(d + 1) * C],
                                                          op0=ALU.mult, op1=ALU.add)
                last.then_inc(a_added, 1)

            def scale_a(b):
                add_z(b, NCH - 1)
                dve.wait_ge(z_ready, b * NCH + NCH)
                nc.vector.reciprocal(rz[:], z[:]).then_inc(rz_ready, 1)
                dve.wait_ge(rz_ready, b + 1)
                nc.vector.tensor_tensor(alpha_rz[:], alpha[:, NCH - 1, :], rz[:],
                                        ALU.mult).then_inc(alpha_rz_ready, 1)
                dve.wait_ge(alpha_rz_ready, b + 1)
                dve.wait_ge(a_added, b * (NCH - 1) + (NCH - 1))
                for d in range(CB):
                    last = nc.vector.tensor_scalar(acc[:, d, :], acc[:, d, :], alpha_rz[:, d:d + 1], None, ALU.mult)
                last.then_inc(a_scaled, 1)

            def finish_a(b):
                dve.wait_ge(a_scaled, b + 1)
                dve.wait_ge(a_ready, b * NCH + NCH)
                for d in range(CB):
                    nc.vector.scalar_tensor_tensor(out=acc[:, d, :], in0=ps_a[:, (NCH - 1) % 2, d * C:(d + 1) * C],
                                                   scalar=rz[:, d:d + 1], in1=acc[:, d, :],
                                                   op0=ALU.mult, op1=ALU.add).then_inc(a_norm, 1)

            def x_low(b, j):
                dve.wait_ge(x_hi_ready, b * NCH + (j + 1))
                nc.vector.tensor_tensor(x_lo[:, j % 2, :], x_nat[:, j, :], x_hi[:, j % 2, :].bitcast(F32),
                                        ALU.subtract).then_inc(x_lo_ready, 1)

            def attend(b, first):
                for j in range(NCH):
                    if j == 1:
                        e_low(b, 0, 0)
                        e_low(b, 0, 1)
                    chunk_max(b, j)
                    if j >= 2:
                        e_low(b, j - 1, 0)
                    shift(b, j)
                    if j >= 2:
                        e_low(b, j - 1, 1)
                    if j == NCH - 1:
                        x_low(b, j)
                    if j >= 2:
                        add_a(b, j - 2)
                    if j < NCH - 1:
                        x_low(b, j)
                    if j == 1:
                        if first:
                            dve.wait_ge(setup_sb, 4)
                        scale(b)
                add_a(b, NCH - 2)
                e_low(b, NCH - 1, 0)
                e_low(b, NCH - 1, 1)

            def take_u(b):
                for c in range(CB):
                    dve.wait_ge(u_ps, b * CB + (c + 1))
                    last = nc.vector.scalar_tensor_tensor(out=u_sb[:, c, :], in0=wq_sum[:],
                                                          scalar=neg_mean[:, c:c + 1],
                                                          in1=ps_a[:, c, 0:C],
                                                          op0=ALU.mult, op1=ALU.add)
                last.then_inc(u_ready, 1)

            def take_m(b):
                for i in range(CB):
                    dve.wait_ge(m_ps, b * CB + (i + 1))
                    last = nc.vector.scalar_tensor_tensor(out=m_full[:, i, :], in0=ps_a[:, i, 0:C],
                                                          scalar=rstd[:, i:i + 1], in1=eye[i],
                                                          op0=ALU.mult, op1=ALU.add)
                last.then_inc(m_full_ready, 1)
                dve.wait_ge(m_full_ready, b + 1)
                nc.vector.tensor_copy(m_hi[:], m_full[:]).then_inc(m_hi_ready, 1)
                dve.wait_ge(m_hi_ready, b + 1)
                nc.vector.tensor_tensor(m_lo[:], m_full[:], m_hi[:].bitcast(F32), ALU.subtract).then_inc(m_ready, 1)

            def bias_row(b, first):
                dve.wait_ge(bias_ps, b + 1)
                if not first:
                    dve.wait_ge(o_ready, b * NCH)
                nc.vector.tensor_tensor(bias[:], ps_k[:, 1, 0, 0:C], b_tile[:], ALU.add).then_inc(bias_ready, 1)

            def emit(b, p):
                dve.wait_ge(r_ready, b * NCH + (p + 1))
                if p == 0:
                    dve.wait_ge(bias_ready, b + 1)
                dve.wait_ge(stored[p % 2], b * (16 * NCH // 2) + 16 * (p // 2))
                nc.vector.tensor_tensor(o_stage[:, p % 2, :].rearrange("p (g t c) -> p g t c", g=2, c=C),
                                        ps_result(p, last_image=True).rearrange("p g (t c) -> p g t c", c=C),
                                        bias[:].unsqueeze(1).unsqueeze(1).broadcast_to([P, 2, TILES // 2, C]),
                                        ALU.add).then_inc(o_ready, 1)

            for p in range(NCH - 1):
                stats_0(p)
            dve.wait_ge(setup_sb, 1)
            stats(0, 0, first=True)

            def period(b, parity, first=False, last=False):
                attend(b, first)
                scale_a(b)
                if not last:
                    turn(b + 1, 1 - parity, 0)
                finish_a(b)
                if not last:
                    turn_stats(b + 1, 1)
                if first:
                    dve.wait_ge(setup_sb, 6)
                take_u(b)
                if not last:
                    turn_low(b + 1, 1 - parity, 1)
                take_m(b)
                if not last:
                    turn(b + 1, 1 - parity, 2)
                    turn_stats(b + 1, 3)
                bias_row(b, first)
                if not last:
                    turn_low(b + 1, 1 - parity, 3)
                    for n in range(4, NCH - 1):
                        turn(b + 1, 1 - parity, n)
                    stats(b + 1, 1 - parity)

            period(0, 0, first=True)
            image_pairs(dve, period)
            period(B - 1, 1, last=True)
            for p in range(NCH):
                emit(B - 1, p)


_INS = ["x", "L0_conv_W_qkv", "L0_conv_W_out", "L0_conv_b_out"]


def kernel(**inputs):
    import numpy as np
    import concourse.bacc as bacc
    from concourse.bass_utils import run_bass_kernel_spmd

    nc = bacc.Bacc("TRN2", target_bir_lowering=False, num_devices=1)
    arrays, args = {}, []
    for name in _INS:
        a = np.ascontiguousarray(inputs[name])
        arrays[f"in_{name}_dram"] = a
        args.append(nc.dram_tensor(f"in_{name}_dram", a.shape, mybir.dt.from_np(a.dtype), kind="ExternalInput").ap())
    o = nc.dram_tensor("out_0_dram", inputs["x"].shape, F32, kind="ExternalOutput").ap()
    build(nc, *args, o)
    r = run_bass_kernel_spmd(nc, [arrays], core_ids=[0])
    return r.results[0]["out_0_dram"]
```
